# Optimizing a Trainium2 kernel written in Bass

```python
import numpy as np
import jax
import jax.numpy as jnp

def _softmax(x, axis=-1):
    return jax.nn.softmax(x, axis=axis)

def _gelu(x):
    return jax.nn.gelu(x, approximate=True)

def _silu(x):
    return jax.nn.silu(x)

def _sigmoid(x):
    return jax.nn.sigmoid(x)

def _layernorm(x, axis=-1, eps=1e-05):
    m = jnp.mean(x, axis=axis, keepdims=True)
    v = jnp.var(x, axis=axis, keepdims=True)
    return (x - m) / jnp.sqrt(v + eps)

def _scatter_add(tgt, idx, src, axis=0):
    return tgt.at[idx].add(src)

def _segment_sum(src, seg, n):
    return jax.ops.segment_sum(src, seg, n)
kernel_name = 'mk_lm_tower_d1_tok_ids1024_r4_8f4f24'

def setup_inputs(seed: int=0):
    np.random.seed(seed)
    _w = jnp.asarray

    def _rec_inputs():
        import jax
        import jax.numpy as jnp
        _rk = jax.random.key(seed)
        x = jax.random.randint(jax.random.fold_in(_rk, 1), (16, 512), 0, 8000, jnp.int32)
        return x
    x = _rec_inputs()

    def _L0_tok_setup():
        import jax, jax.numpy as jnp
        import numpy as np
        MAX_SEQ_LEN = 512
        D_MODEL = 256
        VOCAB = 8000

        def sinusoidal_pe(max_seq_len, d_model, dtype=jnp.float32):
            pos = jnp.arange(max_seq_len, dtype=dtype)[:, None]
            i = jnp.arange(d_model)
            denom = jnp.power(jnp.asarray(10000.0, dtype), (2 * (i // 2)).astype(dtype) / d_model)
            angle = pos / denom
            pe = jnp.where(i % 2 == 0, jnp.sin(angle), jnp.cos(angle))
            return pe
        key = jax.random.key(seed)
        k1, k2 = jax.random.split(key)
        tokens = jax.random.randint(k1, (16, MAX_SEQ_LEN), 0, VOCAB, dtype=jnp.int64 if jax.config.jax_enable_x64 else jnp.int32)
        emb = jax.random.normal(k2, (VOCAB, D_MODEL), dtype=jnp.float32)
        return {'tokens': tokens, 'emb': emb}
    _L0_tok_all = _L0_tok_setup()
    _L0_tok_in = {k: v for k, v in _L0_tok_all.items() if k in ('emb',)}
    del _L0_tok_all

    def _L0_attn_setup():
        import jax, jax.numpy as jnp
        import numpy as np
        E = 256
        H = 16
        HD = E // H
        R = 8
        T, B = (512, 2)

        def _dora_linear(x, m, V, A, Bm, b):
            Vu = V + Bm @ A
            W = m / (jnp.linalg.norm(Vu) + 1e-08) * Vu
            return x @ W.T + b
        key = jax.random.key(seed)
        ks = jax.random.split(key, 16)
        query = jax.random.normal(ks[0], (T, B, E), dtype=jnp.float32)
        kk = jax.random.normal(ks[1], (T, B, E), dtype=jnp.float32)
        vv = jax.random.normal(ks[2], (T, B, E), dtype=jnp.float32)

        def make_dora(k1, k2, k3, k4):
            w = jax.random.normal(k1, (E, E), dtype=jnp.float32) * E ** (-0.5)
            m = jnp.linalg.norm(w)
            V = w / m
            A = jax.random.normal(k2, (R, E), dtype=jnp.float32) * E ** (-0.5)
            Bm = jax.random.normal(k3, (E, R), dtype=jnp.float32) * 0.01
            b = jax.random.normal(k4, (E,), dtype=jnp.float32) * 0.01
            return (m, V, A, Bm, b)
        mag_q, dir_q, A_q, B_q, bias_q = make_dora(ks[3], ks[4], ks[5], ks[6])
        mag_v, dir_v, A_v, B_v, bias_v = make_dora(ks[7], ks[8], ks[9], ks[10])
        k_w = jax.random.normal(ks[11], (E, E), dtype=jnp.float32) * E ** (-0.5)
        k_b = jax.random.normal(ks[12], (E,), dtype=jnp.float32) * 0.01
        out_w = jax.random.normal(ks[13], (E, E), dtype=jnp.float32) * E ** (-0.5)
        out_b = jax.random.normal(ks[14], (E,), dtype=jnp.float32) * 0.01
        return dict(query=query, key=kk, value=vv, mag_q=mag_q, dir_q=dir_q, A_q=A_q, B_q=B_q, bias_q=bias_q, mag_v=mag_v, dir_v=dir_v, A_v=A_v, B_v=B_v, bias_v=bias_v, k_w=k_w, k_b=k_b, out_w=out_w, out_b=out_b)
    _L0_attn_all = _L0_attn_setup()
    _L0_attn_in = {k: v for k, v in _L0_attn_all.items() if k in ('key', 'value', 'mag_q', 'dir_q', 'A_q', 'B_q', 'bias_q', 'mag_v', 'dir_v', 'A_v', 'B_v', 'bias_v', 'k_w', 'k_b', 'out_w', 'out_b')}
    del _L0_attn_all

    def _L0_ffn_setup():
        import jax, jax.numpy as jnp
        import numpy as np
        E, TOPK, R = (8, 2, 16)
        D, H, GH = (256, 16, 64)
        HD = D // H
        SCALE = HD ** (-0.5)

        def _svd_moe(x, Wm, U, S, V, b, idx, gates):
            main = jnp.einsum('bsd,od->bso', x, Wm)
            Ug, Sg, Vg = (U[idx], S[idx], V[idx])
            xv = jnp.einsum('bsd,bkrd->bksr', x, Vg)
            xvs = xv * Sg[:, :, None, :]
            eo = jnp.einsum('bksr,bkor->bkso', xvs, Ug)
            expert = jnp.einsum('bkso,bk->bso', eo, gates)
            return main + expert + b
        key = jax.random.key(seed)
        ks = jax.random.split(key, 32)
        B, S = (32, 257)
        inp = {'hidden_states': jax.random.normal(ks[0], (B, S, D), jnp.float32)}
        inp['gw1'] = jax.random.normal(ks[1], (GH, D), jnp.float32) * 0.02
        inp['gb1'] = jnp.zeros((GH,), jnp.float32)
        inp['gw2'] = jax.random.normal(ks[2], (E, GH), jnp.float32) * 0.02
        inp['gb2'] = jnp.zeros((E,), jnp.float32)
        i = 3
        for p in ('q', 'k', 'v', 'o'):
            inp[p + 'Wm'] = jax.random.normal(ks[i], (D, D), jnp.float32) * 0.02
            i += 1
            inp[p + 'U'] = jax.random.normal(ks[i], (E, D, R), jnp.float32) * 0.02
            i += 1
            inp[p + 'S'] = jax.random.normal(ks[i], (E, R), jnp.float32) * 0.1
            i += 1
            inp[p + 'V'] = jax.random.normal(ks[i], (E, R, D), jnp.float32) * 0.02
            i += 1
            inp[p + 'b'] = jnp.zeros((D,), jnp.float32)
        return inp
    _L0_ffn_all = _L0_ffn_setup()
    _L0_ffn_in = {k: v for k, v in _L0_ffn_all.items() if k in ('gw1', 'gb1', 'gw2', 'gb2', 'qWm', 'qU', 'qS', 'qV', 'qb', 'kWm', 'kU', 'kS', 'kV', 'kb', 'vWm', 'vU', 'vS', 'vV', 'vb', 'oWm', 'oU', 'oS', 'oV', 'ob')}
    del _L0_ffn_all
    return {'x': x, 'L0_tok_emb': _L0_tok_in['emb'], 'L0_attn_key': _L0_attn_in['key'], 'L0_attn_value': _L0_attn_in['value'], 'L0_attn_mag_q': _L0_attn_in['mag_q'], 'L0_attn_dir_q': _L0_attn_in['dir_q'], 'L0_attn_A_q': _L0_attn_in['A_q'], 'L0_attn_B_q': _L0_attn_in['B_q'], 'L0_attn_bias_q': _L0_attn_in['bias_q'], 'L0_attn_mag_v': _L0_attn_in['mag_v'], 'L0_attn_dir_v': _L0_attn_in['dir_v'], 'L0_attn_A_v': _L0_attn_in['A_v'], 'L0_attn_B_v': _L0_attn_in['B_v'], 'L0_attn_bias_v': _L0_attn_in['bias_v'], 'L0_attn_k_w': _L0_attn_in['k_w'], 'L0_attn_k_b': _L0_attn_in['k_b'], 'L0_attn_out_w': _L0_attn_in['out_w'], 'L0_attn_out_b': _L0_attn_in['out_b'], 'L0_ffn_gw1': _L0_ffn_in['gw1'], 'L0_ffn_gb1': _L0_ffn_in['gb1'], 'L0_ffn_gw2': _L0_ffn_in['gw2'], 'L0_ffn_gb2': _L0_ffn_in['gb2'], 'L0_ffn_qWm': _L0_ffn_in['qWm'], 'L0_ffn_qU': _L0_ffn_in['qU'], 'L0_ffn_qS': _L0_ffn_in['qS'], 'L0_ffn_qV': _L0_ffn_in['qV'], 'L0_ffn_qb': _L0_ffn_in['qb'], 'L0_ffn_kWm': _L0_ffn_in['kWm'], 'L0_ffn_kU': _L0_ffn_in['kU'], 'L0_ffn_kS': _L0_ffn_in['kS'], 'L0_ffn_kV': _L0_ffn_in['kV'], 'L0_ffn_kb': _L0_ffn_in['kb'], 'L0_ffn_vWm': _L0_ffn_in['vWm'], 'L0_ffn_vU': _L0_ffn_in['vU'], 'L0_ffn_vS': _L0_ffn_in['vS'], 'L0_ffn_vV': _L0_ffn_in['vV'], 'L0_ffn_vb': _L0_ffn_in['vb'], 'L0_ffn_oWm': _L0_ffn_in['oWm'], 'L0_ffn_oU': _L0_ffn_in['oU'], 'L0_ffn_oS': _L0_ffn_in['oS'], 'L0_ffn_oV': _L0_ffn_in['oV'], 'L0_ffn_ob': _L0_ffn_in['ob']}

def reference(x, L0_tok_emb, L0_attn_key, L0_attn_value, L0_attn_mag_q, L0_attn_dir_q, L0_attn_A_q, L0_attn_B_q, L0_attn_bias_q, L0_attn_mag_v, L0_attn_dir_v, L0_attn_A_v, L0_attn_B_v, L0_attn_bias_v, L0_attn_k_w, L0_attn_k_b, L0_attn_out_w, L0_attn_out_b, L0_ffn_gw1, L0_ffn_gb1, L0_ffn_gw2, L0_ffn_gb2, L0_ffn_qWm, L0_ffn_qU, L0_ffn_qS, L0_ffn_qV, L0_ffn_qb, L0_ffn_kWm, L0_ffn_kU, L0_ffn_kS, L0_ffn_kV, L0_ffn_kb, L0_ffn_vWm, L0_ffn_vU, L0_ffn_vS, L0_ffn_vV, L0_ffn_vb, L0_ffn_oWm, L0_ffn_oU, L0_ffn_oS, L0_ffn_oV, L0_ffn_ob):
    import jax
    import jax.numpy as jnp

    def _L0_tok_ref(tokens, emb):
        import jax, jax.numpy as jnp
        import numpy as np
        MAX_SEQ_LEN = 512
        D_MODEL = 256
        VOCAB = 8000

        def sinusoidal_pe(max_seq_len, d_model, dtype=jnp.float32):
            pos = jnp.arange(max_seq_len, dtype=dtype)[:, None]
            i = jnp.arange(d_model)
            denom = jnp.power(jnp.asarray(10000.0, dtype), (2 * (i // 2)).astype(dtype) / d_model)
            angle = pos / denom
            pe = jnp.where(i % 2 == 0, jnp.sin(angle), jnp.cos(angle))
            return pe
        we = jnp.take(emb, tokens, axis=0)
        pe = sinusoidal_pe(MAX_SEQ_LEN, D_MODEL, we.dtype)
        return we + pe[None, :, :]

    def _L0_attn_ref(query, key, value, mag_q, dir_q, A_q, B_q, bias_q, mag_v, dir_v, A_v, B_v, bias_v, k_w, k_b, out_w, out_b):
        import jax, jax.numpy as jnp
        import numpy as np
        E = 256
        H = 16
        HD = E // H
        R = 8
        T, B = (512, 2)

        def _dora_linear(x, m, V, A, Bm, b):
            Vu = V + Bm @ A
            W = m / (jnp.linalg.norm(Vu) + 1e-08) * Vu
            return x @ W.T + b
        Tq, Bq, _ = query.shape
        q = _dora_linear(query, mag_q, dir_q, A_q, B_q, bias_q)
        k = query @ k_w.T + k_b
        v = _dora_linear(query, mag_v, dir_v, A_v, B_v, bias_v)
        q = q.reshape(Tq, Bq * H, HD).transpose(1, 0, 2)
        k = k.reshape(Tq, Bq * H, HD).transpose(1, 0, 2)
        v = v.reshape(Tq, Bq * H, HD).transpose(1, 0, 2)
        scale = HD ** (-0.5)
        attn = jnp.einsum('nqd,nkd->nqk', q, k) * scale
        attn = jax.nn.softmax(attn, axis=-1)
        out = jnp.einsum('nqk,nkd->nqd', attn, v)
        out = out.transpose(1, 0, 2).reshape(Tq, Bq, E)
        out = out @ out_w.T + out_b
        return out

    def _L0_ffn_ref(hidden_states, gw1, gb1, gw2, gb2, qWm, qU, qS, qV, qb, kWm, kU, kS, kV, kb, vWm, vU, vS, vV, vb, oWm, oU, oS, oV, ob):
        import jax, jax.numpy as jnp
        import numpy as np
        E, TOPK, R = (8, 2, 16)
        D, H, GH = (256, 16, 64)
        HD = D // H
        SCALE = HD ** (-0.5)

        def _svd_moe(x, Wm, U, S, V, b, idx, gates):
            main = jnp.einsum('bsd,od->bso', x, Wm)
            Ug, Sg, Vg = (U[idx], S[idx], V[idx])
            xv = jnp.einsum('bsd,bkrd->bksr', x, Vg)
            xvs = xv * Sg[:, :, None, :]
            eo = jnp.einsum('bksr,bkor->bkso', xvs, Ug)
            expert = jnp.einsum('bkso,bk->bso', eo, gates)
            return main + expert + b
        B, S, _ = hidden_states.shape
        pooled = hidden_states.mean(axis=1)
        h = jax.nn.relu(pooled @ gw1.T + gb1)
        logits = h @ gw2.T + gb2
        top_vals, top_idx = jax.lax.top_k(logits, TOPK)
        gates = jax.nn.softmax(top_vals, axis=-1)
        q = _svd_moe(hidden_states, qWm, qU, qS, qV, qb, top_idx, gates) * SCALE
        k = _svd_moe(hidden_states, kWm, kU, kS, kV, kb, top_idx, gates)
        v = _svd_moe(hidden_states, vWm, vU, vS, vV, vb, top_idx, gates)

        def shp(t):
            return t.reshape(B, S, H, HD).transpose(0, 2, 1, 3)
        q, k, v = (shp(q), shp(k), shp(v))
        attn = jax.nn.softmax(jnp.einsum('bhsd,bhtd->bhst', q, k), axis=-1)
        ctx = jnp.einsum('bhst,bhtd->bhsd', attn, v)
        ctx = ctx.transpose(0, 2, 1, 3).reshape(B, S, D)
        out = _svd_moe(ctx, oWm, oU, oS, oV, ob, top_idx, gates)
        return out
    h = _L0_tok_ref(x, L0_tok_emb)
    h = h + _L0_attn_ref(_layernorm(h, axis=-1), L0_attn_key, L0_attn_value, L0_attn_mag_q, L0_attn_dir_q, L0_attn_A_q, L0_attn_B_q, L0_attn_bias_q, L0_attn_mag_v, L0_attn_dir_v, L0_attn_A_v, L0_attn_B_v, L0_attn_bias_v, L0_attn_k_w, L0_attn_k_b, L0_attn_out_w, L0_attn_out_b)
    h = h + _L0_ffn_ref(_layernorm(h, axis=-1), L0_ffn_gw1, L0_ffn_gb1, L0_ffn_gw2, L0_ffn_gb2, L0_ffn_qWm, L0_ffn_qU, L0_ffn_qS, L0_ffn_qV, L0_ffn_qb, L0_ffn_kWm, L0_ffn_kU, L0_ffn_kS, L0_ffn_kV, L0_ffn_kb, L0_ffn_vWm, L0_ffn_vU, L0_ffn_vS, L0_ffn_vV, L0_ffn_vb, L0_ffn_oWm, L0_ffn_oU, L0_ffn_oS, L0_ffn_oV, L0_ffn_ob)
    return h

_drawn_inputs = setup_inputs


def setup_inputs(seed=0):
    import zlib

    import numpy as np

    out = dict(_drawn_inputs(seed))
    spreads = {'L0_ffn_gb1': (0.0, 0.8),
     'L0_ffn_gb2': (0.0, 0.8),
     'L0_ffn_qb': (0.0, 0.8),
     'L0_ffn_kb': (0.0, 0.8),
     'L0_ffn_vb': (0.0, 0.392),
     'L0_ffn_ob': (0.0, 0.1)}
    factors = {'L0_attn_bias_q': 8.0,
     'L0_attn_bias_v': 7.927,
     'L0_attn_k_b': 8.0,
     'L0_attn_out_b': 8.0,
     'L0_ffn_gw1': 8.0,
     'L0_ffn_gw2': 8.0,
     'L0_ffn_qWm': 8.0,
     'L0_ffn_qU': 8.0,
     'L0_ffn_qS': 8.0,
     'L0_ffn_qV': 8.0,
     'L0_ffn_kWm': 8.0,
     'L0_ffn_kU': 8.0,
     'L0_ffn_kS': 8.0,
     'L0_ffn_kV': 8.0,
     'L0_ffn_vU': 8.0,
     'L0_ffn_vS': 8.0,
     'L0_ffn_vV': 8.0,
     'L0_ffn_oU': 8.0,
     'L0_ffn_oS': 8.0,
     'L0_ffn_oV': 8.0}
    for name, (base, spread) in spreads.items():
        noise = np.random.default_rng([zlib.crc32(name.encode()), seed]).standard_normal(out[name].shape)
        drawn = base * np.exp(spread * noise) if base else spread * noise
        out[name] = jnp.asarray(drawn.astype(out[name].dtype))
    for name, factor in factors.items():
        out[name] = (out[name] * factor).astype(out[name].dtype)
    return out
```

```python
from contextlib import ExitStack

import numpy as np
import concourse.bass as bass
from concourse import mybir

F32, BF16, I32, U32 = mybir.dt.float32, mybir.dt.bfloat16, mybir.dt.int32, mybir.dt.uint32
ALU, ACT, AX = mybir.AluOpType, mybir.ActivationFunctionType, mybir.AxisListType

P = 128
BATCH, SEQ, D = 16, 512, 256
HEADS, HD = 16, 16
EXPERTS, RANK, GATE_H = 8, 16, 64
DORA_R = 8
TOK = 512
NT = TOK // P
ITEMS = BATCH * SEQ // TOK
KC = D // P
GROUPS, GH = 4, 4
SPLIT = 96
MASK0, MAX0, KALL = 96, 104, 106
SCALE = HD ** -0.5
EPS = 1e-5
FAR = 2.0 ** 40
PARTS_Q = (0, 1, 2, 0, 1, 0)
PARTS_K = (0, 0, 0, 1, 1, 2)
NPROB = 8


class Phase:


    def __init__(self, second):
        self.second = second
        self.blocks = 16 if second else 4
        self.steps = self.blocks // 4
        self.bank_of = dict(x="T", m="T", q0="A", k0="B", ct1="A", o0="B", o1="A", wo="B", q1="A", k1="B",
                            ct0="B", v0="A", v1="B", t0="A", t1="B", wq="A", wk="B", wv="A", pl="B")
        self.chain = dict(ms=1, x=1, pn=0 if second else 17, ln=0 if second else 17)
        self.use, self.chained = {}, {}
        count = {"T": 0, "A": 0, "B": 0}
        links = 0
        for n in range(-1, ITEMS + 1):
            for tok in self.tokens(n):
                kind, m, x = tok
                if kind in self.bank_of:
                    count[self.bank_of[kind]] += 1
                    self.use[kind, m, x] = count[self.bank_of[kind]]
                if kind == "M" and x[1] == self.blocks - 1:
                    self.chained["ms", m, x[0]] = links
                    links += self.chain["ms"]
                elif kind in self.chain:
                    self.chained[kind, m, x] = links
                    links += self.chain[kind]

    def tokens(self, n):
        have = lambda m: 0 <= m < ITEMS
        w = lambda m, *names: [(x, m, 0) for x in names] if self.second and have(m) else []
        if n == -1:
            prepare = lambda m: [(x, m, 0) for x in ("prep", "pg", "pa", "ps", "pn", "t0", "t1")]
            out = prepare(0) + w(0, "wq", "wk", "wv")
            out += [("q0", 0, 0), ("k0", 0, 0), ("sw", 0, 0), ("q1", 0, 0), ("k1", 0, 0), ("sw", 0, 1)]
            out += [("sr", 0, 0), ("sr", 0, 1), ("v0", 0, 0), ("v1", 0, 0), ("vc", 0, 0), ("vc", 0, 1), ("vc", 0, 2)]
            out += [("sr", 0, 2)] + prepare(1) + w(1, "wq", "wk", "wv")
            out += [("M", 0, (g, k)) for g in range(2) for k in range(self.blocks)]
            return out + [("m", 0, 0)]
        if n == ITEMS:
            out = [("pv", n - 1, (3, self.steps - 1)), ("x", n - 1, 3), ("ct1", n - 1, 0), ("o0", n - 1, 0), ("o1", n - 1, 0)]
            return out + ([] if self.second else [("ln", n - 1, 0), ("pl", n - 1, 0)]) + [("st", n - 1, 0), ("s2", n - 1, 0)]
        out = []
        for g in range(GROUPS):
            ahead = lambda d: (n + (g + d) // 4, (g + d) % 4)
            items, late = [], []
            if g > 0:
                before = (n, g - 1)
            else:
                before = (n - 1, 3)
            if have(ahead(1)[0]):
                items.append(("m", *ahead(1)))
            if have(before[0]):
                items.append(("x", *before))
            if g == 0:
                items.append(("vc", n, 3))
                if have(n + 1):
                    items += [("q0", n + 1, 0), ("k0", n + 1, 0)]
                    late = [("sw", n + 1, 0)]
                if have(n + 2):
                    items.insert(0, ("prep", n + 2, 0))
                    late.append(("pg", n + 2, 0))
            if g == 1:
                if n >= 1:
                    items += [("ct1", n - 1, 0), ("o0", n - 1, 0), ("o1", n - 1, 0)]
                    items += [] if self.second else [("ln", n - 1, 0)]
                    late = [("st", n - 1, 0)]
                items += w(n, "wo")
                if have(n + 2):
                    late.append(("pa", n + 2, 0))
            if g == 2:
                items.append(("rs", n, 0))
                if have(n + 1):
                    items += [("q1", n + 1, 0), ("k1", n + 1, 0)]
                    late = [("sw", n + 1, 1)]
                if n >= 1:
                    items.append(("s2", n - 1, 0))
                if have(n + 2):
                    late += [("ps", n + 2, 0), ("pn", n + 2, 0)]
                late.append(("rb", n, 0))
            if g == 3:
                items.append(("ct0", n, 0))
                if have(n + 1):
                    items += [("v0", n + 1, 0), ("v1", n + 1, 0)]
                    late = [("vc", n + 1, i) for i in range(3)]
                if not self.second and n >= 1:
                    items.append(("pl", n - 1, 0))
                if have(n + 2):
                    items += [("t0", n + 2, 0), ("t1", n + 2, 0)] + w(n + 2, "wq", "wk", "wv")
            if have(ahead(3)[0]):
                items.insert(2 if g == 0 and have(n + 2) else 1, ("sr", *ahead(3)))
            done = 0
            for k in range(self.blocks):
                out.append(("s", n, (g, k)))
                if k % 4 == 1:
                    step = g * self.steps + k // 4 - 1
                    if step >= 0:
                        out.append(("pv", n, (step // self.steps, step % self.steps)))
                    elif n > 0:
                        out.append(("pv", n - 1, (3, self.steps - 1)))
                if have(ahead(2)[0]):
                    out.append(("M", ahead(2)[0], (ahead(2)[1], k)))
                if k >= 1:
                    upto = (k * len(items)) // (self.blocks - 1)
                    out += items[done:upto]
                    done = upto
            out += late
        return out

    def run(self, engine, handlers):
        def emit(template, reg):
            for kind, m, x in self.tokens(template):
                if kind not in handlers:
                    continue
                if reg is None:
                    value = lambda f, m=m: f(m)
                    item = m
                else:
                    def value(f, m=m):
                        a, b = f(m), f(m + 1)
                        assert a > 0 and f(m + ITEMS - 5) == a + (b - a) * (ITEMS - 5), kind
                        return reg * (b - a) + (a - 2 * (b - a)) if b != a else a
                    item = reg + (m - 2) if m != 2 else reg
                if isinstance(x, tuple):
                    handlers[kind](item, value, *x)
                else:
                    handlers[kind](item, value, x)
        emit(-1, None)
        emit(0, None)
        emit(1, None)
        with engine.Fori(2, ITEMS - 2) as n:
            emit(2, n)
        emit(ITEMS - 2, None)
        emit(ITEMS - 1, None)
        emit(ITEMS, None)


def tower(nc, ctx, io, out):
    sb = lambda name, shape, dt: ctx.enter_context(nc.sbuf_tensor(name, shape, dt))
    ps = lambda name: ctx.enter_context(nc.psum_tensor(name, [P, 512], F32))
    sem = lambda name: ctx.enter_context(nc.semaphore(name))
    dram = lambda name, shape, dt: nc.dram_tensor(name, shape, dt, kind="Internal").ap()

    h0_dram = dram("h0_rows", [ITEMS, P, NT, D], F32)
    h1_dram = dram("h1_rows", [SEQ * BATCH, D], F32)
    xn_dram = dram("xn_rows", [SEQ * BATCH, D], F32)
    qs_dram = dram("q_parts", [2, 3 * HD, 8, TOK], BF16)
    ks_dram = dram("k_stack", [2, SPLIT, 8, TOK], BF16)
    by_batch = lambda t: t.rearrange("(i p b) c -> b p i c", p=P, b=BATCH)
    by_item = lambda t: t.rearrange("(n i p) c -> n p i c", p=P, i=NT)

    qstack = sb("qstack", [P, GROUPS, GH, TOK], BF16)
    kstack = sb("kstack", [P, GROUPS, GH, TOK], BF16)
    prob = sb("prob", [P, NPROB, TOK], F32)
    vp = sb("vp", [P, NT, HEADS, 32], F32)
    vs = sb("vs", [P, NT, D], F32)
    xn = sb("xn", [P, NT, D], F32)
    hnT = sb("hnT", [P, KC, TOK], F32)
    ctxS = sb("ctxS", [P, TOK], F32)
    ctxn = sb("ctxn", [P, NT, D], F32)
    ctxT = sb("ctxT", [P, KC, TOK], F32)
    res = sb("res", [P, NT, D], F32)
    hout = sb("hout", [P, NT, D], F32)
    hnew = sb("hnew", [P, NT, D], F32)
    part = {(a, c, i): sb(f"part_{a}{c}{i}", [P, TOK], BF16) for a in "qk" for c in range(2) for i in range(3)}
    rest = {a: sb(f"rest_{a}", [P, TOK], F32) for a in "qk"}
    W = {a: sb(f"w_{a}", [P, KC, D], F32) for a in "qkvo"}
    mf = sb("mf", [P, NT, GH], F32)
    mh = sb("mh", [P, NT, 2, GH], BF16)
    mrow = sb("mrow", [2 * GH, TOK], BF16)
    rden = sb("rden", [P, NT, GH], F32)
    emb_t = sb("emb_t", [P, NT, D], F32)
    pe_t = sb("pe_t", [P, NT, D], F32)
    idx_t = sb("idx_t", [P, NT], I32)
    stats = {a: sb(f"stats_{a}", [P, NT, 6], F32) for a in ("pn", "ln")}
    aggr = {a: sb(f"aggr_{a}", [P, NT, 2], F32) for a in ("pn", "ln")}
    root = {a: sb(f"root_{a}", [P, 4, NT], F32) for a in ("pn", "ln")}
    ident = sb("ident", [P, P], F32)
    identb = sb("identb", [P, P], BF16)
    ones = sb("ones", [P, P], F32)
    mean_sel = sb("mean_sel", [P, BATCH], F32)
    pooled = sb("pooled", [P, KC, BATCH], F32)
    bias_col = {(f, a): sb(f"bias_{f}{a}", [P, KC], F32) for f in "af" for a in "qk"}
    bias_row = {(f, a): sb(f"bias_{f}{a}", [P, D], F32) for f in "af" for a in "vo"}
    main = {a: sb(f"main_{a}", [P, KC, D], F32) for a in "qkvo"}
    vall = {a: sb(f"vall_{a}", [P, D], F32) for a in "qkvo"}
    uall = {a: sb(f"uall_{a}", [P, D], F32) for a in "qkvo"}
    uc = {a: sb(f"uc_{a}", [P, D], F32) for a in "qkvo"}
    sall = sb("sall", [P, 4], F32)
    coef = sb("coef", [P, BATCH, 4], F32)
    coef_b = {a: sb(f"coef_{a}", [P, 1], F32) for a in "qkvo"}

    sc = [ps("sc0"), ps("sc1")]
    mx = [ps("mx0"), ps("mx1")]
    ctxp = ps("ctxp")
    bank = {"T": ps("bankT"), "A": ps("bankA"), "B": ps("bankB")}

    def rsqrt(eng, link, dst, var, tmp, magic, y):
        link(eng.tensor_scalar(magic, var.bitcast(I32), 1, None, ALU.logical_shift_right))
        link(eng.tensor_scalar(y.bitcast(I32), magic, -1.0, float(0x5F3759DF), ALU.mult, ALU.add))
        for i in range(3):
            link(eng.tensor_tensor(tmp, y, y, ALU.mult))
            link(eng.tensor_tensor(tmp, tmp, var, ALU.mult))
            link(eng.tensor_scalar(tmp, tmp, -0.5, 1.5, ALU.mult, ALU.add))
            to = dst if i == 2 else y
            last = eng.tensor_tensor(to, y, tmp, ALU.mult)
            if i < 2:
                link(last)
        return last

    def setup():
        A_t = {a: sb(f"dora_a_{a}", [DORA_R, D], F32) for a in "qv"}
        Bt_t = {a: sb(f"dora_b_{a}", [DORA_R, D], F32) for a in "qv"}
        mag = sb("mag", [P, 2], F32)
        sq = sb("sq", [P, 2, D * KC], F32)
        ssum = sb("ssum", [P, 2], F32)
        tot = sb("tot", [P, 2], F32)
        tmp3 = sb("tmp3", [P, 3, 2], F32)
        s_w, s_set, s_pe, s_chain, s_pool = sem("su_loads"), sem("su_ready"), sem("su_products"), sem("su_chain"), sem("su_pool")
        with nc.Block() as block:
            @block.sync
            def _(sp):
                n = 0
                loads = [(ident[:], io["c_ident"]), (mean_sel[:], io["c_mean"])]
                half = lambda w: w.rearrange("(c p) o -> p c o", p=P)
                loads += [(W["q"][:], half(io["a_dir_qT"])), (W["v"][:], half(io["a_dir_vT"]))]
                loads += [(W["k"][:], half(io["a_k_wT"])), (W["o"][:], half(io["a_out_wT"]))]
                for i, a in enumerate("qv"):
                    loads += [(A_t[a][:], io[f"a_A_{a}"]), (Bt_t[a][:], io[f"a_B_{a}T"])]
                    loads.append((mag[:, i:i + 1], io[f"a_mag_{a}"].to_broadcast([P, 1])))
                for f in "af":
                    for a in "qk":
                        loads.append((bias_col[f, a][:], io[f"{f}_b{a}"].rearrange("(c p) -> p c", p=P)))
                    for a in "vo":
                        loads.append((bias_row[f, a][:], io[f"{f}_b{a}"].rearrange("(a c) -> a c", a=1).to_broadcast([P, D])))
                for i, a in enumerate("qkvo"):
                    loads += [(main[a][:], half(io[f"f_{a}WmT"])), (vall[a][:], io[f"f_{a}V"]), (uall[a][:], io[f"f_{a}UT"])]
                    loads.append((sall[:, i:i + 1], io[f"f_{a}S"]))
                with nc.allow_non_contiguous_dma(reason="a few hundred bytes of biases"):
                    for to, of in loads:
                        sp.dma_start(to, of).then_inc(s_w, 16)
                setup.loads = 16 * len(loads)

            @block.gpsimd
            def _(pool):
                rows = lambda t: t[MASK0:MAX0].rearrange("r g j (i s b) -> r (g j i) s b", s=P // BATCH, b=BATCH)
                same = [[0, GROUPS * GH * NT], [1, P // BATCH], [0, BATCH]]
                pool.wait_ge(s_set, 4)
                nc.gpsimd.affine_select(out=rows(qstack), in_=rows(qstack), compare_op=ALU.not_equal, fill=1.0,
                                        base=0, pattern=same, channel_multiplier=-1).then_inc(s_pool, 1)
                nc.gpsimd.affine_select(out=rows(kstack), in_=rows(kstack), compare_op=ALU.not_equal, fill=0.0,
                                        base=0, pattern=same, channel_multiplier=-1).then_inc(s_pool, 1)

            @block.vector
            def _(dve):
                links = [0]

                def link(ins):
                    links[0] += 1
                    ins.then_inc(s_chain, 1)
                    dve.wait_ge(s_chain, links[0])

                nc.vector.memset(qstack[MASK0:P], 0.0).then_inc(s_set, 1)
                nc.vector.memset(kstack[MASK0:P], 1.0).then_inc(s_set, 1)
                dve.wait_ge(s_set, 2)
                nc.vector.memset(kstack[MASK0:MAX0], -FAR).then_inc(s_set, 1)
                nc.vector.memset(vp[:], 0.0).then_inc(s_set, 1)
                dve.wait_ge(s_set, 4)
                link(nc.vector.memset(vp[:, :, :, HD:HD + 1], 1.0))
                link(nc.vector.memset(ones[:], 1.0))
                link(nc.vector.memset(pooled[:], 0.0))
                dve.wait_ge(s_w, setup.loads)
                link(nc.vector.tensor_copy(identb[:], ident[:]))
                for i, a in enumerate("qv"):
                    for c in range(KC):
                        dve.wait_ge(s_pe, 1)
                        link(nc.vector.tensor_tensor(W[a][:, c, :], sc[i][:, c * D:(c + 1) * D], W[a][:, c, :], ALU.add))
                    flat = W[a][:].rearrange("p c o -> p (c o)")
                    link(nc.vector.tensor_tensor(sq[:, i, :], flat, flat, ALU.mult))
                    nc.vector.tensor_reduce(ssum[:, i:i + 1], sq[:, i, :], AX.X, ALU.add).then_inc(s_set, 1)
                dve.wait_ge(s_pe, 2)
                link(nc.vector.tensor_copy(tot[:], mx[0][:, 0:2]))
                last = rsqrt(nc.vector, link, tmp3[:, 2, :], tot[:], tmp3[:, 0, :], tmp3[:, 1, :].bitcast(I32), ssum[:])
                link(last)
                link(nc.vector.tensor_tensor(tot[:], tot[:], tmp3[:, 2, :], ALU.mult))
                link(nc.vector.tensor_scalar(tot[:], tot[:], 1e-8, None, ALU.add))
                link(nc.vector.reciprocal(tmp3[:, 0, :], tot[:]))
                link(nc.vector.tensor_tensor(tot[:], tmp3[:, 0, :], mag[:], ALU.mult))
                for i, a in enumerate("qv"):
                    link(nc.vector.tensor_scalar(W[a][:], W[a][:], tot[:, i:i + 1], None, ALU.mult))

            @block.tensor
            def _(pe):
                pe.wait_ge(s_w, setup.loads)
                for i, a in enumerate("qv"):
                    for c in range(KC):
                        last = nc.tensor.matmul(sc[i][:, c * D:(c + 1) * D], A_t[a][:, c * P:(c + 1) * P], Bt_t[a][:],
                                                start=True, stop=True)
                last.then_inc(s_pe, 1)
                pe.wait_ge(s_set, 6)
                nc.tensor.matmul(mx[0][:, 0:2], ones[:], ssum[:], start=True, stop=True).then_inc(s_pe, 1)

    def attention(second):
        ph = Phase(second)
        NB = ph.blocks
        pre = "f_" if second else "a_"
        fam = "f" if second else "a"
        s = {x: sem(pre + x) for x in (
            "score_ready", "exp_done", "max_ready", "max_done", "max_split", "pv_done", "ctx_copied",
            "qk_high", "qk_rest", "qk_parts", "v_copied", "chain", "xn_ready", "res_ready", "hout_ready",
            "hnew_ready", "uc_ready", "coef_ready", "waits_done", "pe_added")}
        free = {b: sem(f"{pre}bank{b}_free") for b in bank}
        ready = {b: sem(f"{pre}bank{b}_ready") for b in bank}
        d_write = [sem(f"{pre}d_stack_write{c}") for c in range(2)]
        d_read = [sem(f"{pre}d_stack_read{g}") for g in range(GROUPS)]
        d_max = [sem(f"{pre}d_max_rows{g}") for g in range(GROUPS)]
        d_res, d_x, d_idx, d_pe, d_h0, d_out, d_out2 = (sem(pre + x) for x in (
            "d_res", "d_x", "d_idx", "d_pe", "d_h0", "d_out", "d_out2"))
        slot = lambda m, g: 4 * m + g
        use = lambda kind, x=0: (lambda m: ph.use[kind, m, x])

        uc_order = [(kind[1], m) for n in range(-1, ITEMS + 1) for kind, m, _ in ph.tokens(n) if kind in ("wq", "wk", "wv", "wo")]
        uc_count = lambda m, a: uc_order.index((a, m)) + 1

        def hold(eng, semaphore, count):
            eng.wait_ge(semaphore, count)
            if not isinstance(count, int):
                eng.sem_inc(s["waits_done"])

        def before_use(eng, value, kind, x=0):
            first = value(lambda m: ph.use[kind, m, x] - 1)
            if not (isinstance(first, int) and first == 0):
                eng.wait_ge(free[ph.bank_of[kind]], value(lambda m: ph.use[kind, m, x] - 1))

        def wait_bank(eng, value, kind, x=0):
            eng.wait_ge(ready[ph.bank_of[kind]], value(use(kind, x)))

        with nc.Block() as block:
            @block.tensor
            def _(pe):
                mm = nc.tensor.matmul

                def score(m, value, g, k):
                    t, j = divmod(k, 4)
                    if k == 0:
                        pe.wait_ge(d_read[g], value(lambda m: 64 * (m + 1)))
                        pe.wait_ge(d_max[g], value(lambda m: 32 * (m + 1)))
                    block_no = lambda m: slot(m, g) * NB + k
                    if value(block_no) not in (0, 1) if isinstance(m, int) else True:
                        pe.wait_ge(s["exp_done"], value(lambda m: block_no(m) - 1))
                    to = sc[k % 2]
                    if second:
                        last = mm(to[:], kstack[0:KALL, g, j, t * P:(t + 1) * P], qstack[0:KALL, g, j, :], start=True, stop=True)
                    else:
                        for i in range(NT):
                            cols = slice(i * P, (i + 1) * P)
                            last = mm(to[:, cols], kstack[0:KALL, g, j, cols], qstack[0:KALL, g, j, cols], start=True, stop=True)
                    last.then_inc(s["score_ready"], 1)

                def maximum(m, value, g, k):
                    t, j = divmod(k, 4)
                    if k == 0:
                        pe.wait_ge(d_read[g], value(lambda m: 64 * (m + 1)))
                    block_no = lambda m: slot(m, g) * NB + k
                    if not isinstance(m, int) or block_no(m) > 1:
                        pe.wait_ge(s["max_done"], value(lambda m: block_no(m) - 1))
                    to = mx[k % 2]
                    if second:
                        last = mm(to[:], qstack[0:MAX0, g, j, t * P:(t + 1) * P], kstack[0:MAX0, g, j, :], start=True, stop=True)
                    else:
                        for i in range(NT):
                            cols = slice(i * P, (i + 1) * P)
                            last = mm(to[:, cols], qstack[0:MAX0, g, j, cols], kstack[0:MAX0, g, j, cols], start=True, stop=True)
                    last.then_inc(s["max_ready"], 1)

                def values(m, value, g, step):
                    first = lambda m: (slot(m, g) * ph.steps + step) * 4
                    pe.wait_ge(s["exp_done"], value(lambda m: first(m) + 4))
                    if step == 0:
                        pe.wait_ge(s["v_copied"], value(lambda m: slot(m, g) + 1))
                        if not isinstance(m, int) or slot(m, g) > 0:
                            pe.wait_ge(s["ctx_copied"], value(lambda m: slot(m, g)))
                    at = (g * ph.steps + step) * 4 % NPROB
                    for i in range(1 if second else NT):
                        for j in range(GH):
                            h, cols = g * GH + j, slice(i * P, (i + 1) * P)
                            if second:
                                last = mm(ctxp[32 * j:32 * j + 32, :], vp[:, step, h, :], prob[:, at + j, :],
                                          start=(step == 0), stop=(step == ph.steps - 1))
                            else:
                                last = mm(ctxp[32 * j:32 * j + 32, cols], vp[:, i, h, :], prob[:, at + j, cols],
                                          start=True, stop=True)
                    last.then_inc(s["pv_done"], 1)

                def max_rows(m, value, g):
                    before_use(pe, value, "m", g)
                    pe.wait_ge(s["max_split"], value(lambda m: slot(m, g) + 1))
                    rows = bank["T"][0:2 * GH, :].bitcast(BF16)
                    for i in range(NT):
                        last = nc.tensor.transpose(rows[:, i * P:(i + 1) * P], mh[:, i, :, :].rearrange("p a j -> p (a j)"), identb[:])
                    last.then_inc(ready["T"], 1)

                def turn_context(m, value, g):
                    before_use(pe, value, "x", g)
                    pe.wait_ge(s["ctx_copied"], value(lambda m: slot(m, g) + 1))
                    for i in range(NT):
                        last = nc.tensor.transpose(bank["T"][:, i * P:(i + 1) * P], ctxS[:, i * P:(i + 1) * P], ident[:])
                    last.then_inc(ready["T"], 1)

                def turn_normal(c):
                    def f(m, value, _):
                        before_use(pe, value, f"ct{c}")
                        pe.wait_ge(free["T"], value(use("x", 2 * c + 1)))
                        to = bank[ph.bank_of[f"ct{c}"]]
                        for i in range(NT):
                            last = nc.tensor.transpose(to[:, i * P:(i + 1) * P], ctxn[:, i, c * P:(c + 1) * P], ident[:])
                        last.then_inc(ready[ph.bank_of[f"ct{c}"]], 1)
                    return f

                def turn_tokens(c):
                    def f(m, value, _):
                        before_use(pe, value, f"t{c}")
                        if second:
                            pe.wait_ge(d_x, value(lambda m: 16 * (m + 1)))
                        else:
                            pe.wait_ge(s["xn_ready"], value(lambda m: m + 1))
                        to = bank[ph.bank_of[f"t{c}"]]
                        for i in range(NT):
                            last = nc.tensor.transpose(to[:, i * P:(i + 1) * P], xn[:, i, c * P:(c + 1) * P], ident[:])
                        last.then_inc(ready[ph.bank_of[f"t{c}"]], 1)
                    return f

                def project_t(a, c):
                    def f(m, value, _):
                        before_use(pe, value, f"{a}{c}")
                        if c == 0:
                            pe.wait_ge(free[ph.bank_of["t0"]], value(use("t0")))
                            pe.wait_ge(free[ph.bank_of["t1"]], value(use("t1")))
                            if second:
                                pe.wait_ge(free[ph.bank_of["w" + a]], value(use("w" + a)))
                        to = bank[ph.bank_of[f"{a}{c}"]]
                        for kc in range(KC):
                            last = mm(to[:], W[a][:, kc, c * P:(c + 1) * P], hnT[:, kc, :], start=(kc == 0), stop=(kc == KC - 1))
                        last.then_inc(ready[ph.bank_of[f"{a}{c}"]], 1)
                    return f

                def project(kind, a, half, src):
                    def f(m, value, _):
                        before_use(pe, value, kind)
                        if kind == "v0" and second:
                            pe.wait_ge(free[ph.bank_of["wv"]], value(use("wv")))
                        if kind == "o0":
                            pe.wait_ge(free[ph.bank_of["ct0"]], value(use("ct0")))
                            pe.wait_ge(free[ph.bank_of["ct1"]], value(use("ct1")))
                            if second:
                                pe.wait_ge(free[ph.bank_of["wo"]], value(use("wo")))
                        to = bank[ph.bank_of[kind]]
                        for i in (2 * half, 2 * half + 1):
                            for kc in range(KC):
                                last = mm(to[:, (i % 2) * D:(i % 2 + 1) * D], src[:, kc, i * P:(i + 1) * P], W[a][:, kc, :],
                                          start=(kc == 0), stop=(kc == KC - 1))
                        last.then_inc(ready[ph.bank_of[kind]], 1)
                    return f

                def experts(a):
                    def f(m, value, _):
                        before_use(pe, value, "w" + a)
                        pe.wait_ge(s["uc_ready"], value(lambda m: uc_count(m, a)))
                        to = bank[ph.bank_of["w" + a]]
                        for c in range(KC):
                            last = mm(to[:, c * D:(c + 1) * D], vall[a][:, c * P:(c + 1) * P], uc[a][:], start=True, stop=True)
                        last.then_inc(ready[ph.bank_of["w" + a]], 1)
                    return f

                def pool_tokens(m, value, _):
                    before_use(pe, value, "pl")
                    pe.wait_ge(s["hnew_ready"], value(lambda m: m + 1))
                    to = bank[ph.bank_of["pl"]]
                    for c in range(KC):
                        for i in range(NT):
                            last = mm(to[:, c * BATCH:(c + 1) * BATCH], hnew[:, i, c * P:(c + 1) * P], mean_sel[:],
                                      start=(i == 0), stop=(i == NT - 1))
                    last.then_inc(ready[ph.bank_of["pl"]], 1)

                ph.run(pe, dict(s=score, M=maximum, pv=values, m=max_rows, x=turn_context, ct0=turn_normal(0), ct1=turn_normal(1),
                                t0=turn_tokens(0), t1=turn_tokens(1), q0=project_t("q", 0), k0=project_t("k", 0),
                                q1=project_t("q", 1), k1=project_t("k", 1), v0=project("v0", "v", 0, hnT), v1=project("v1", "v", 1, hnT),
                                o0=project("o0", "o", 0, ctxT), o1=project("o1", "o", 1, ctxT), wq=experts("q"), wk=experts("k"),
                                wv=experts("v"), wo=experts("o"), pl=pool_tokens))

            @block.scalar
            def _(act):
                def exponent(m, value, g, k):
                    block_no = lambda m: slot(m, g) * NB + k
                    at = (g * NB + k) % NPROB
                    act.wait_ge(s["score_ready"], value(lambda m: block_no(m) + 1))
                    if k % 4 == 0 and (not isinstance(m, int) or block_no(m) >= NPROB):
                        act.wait_ge(s["pv_done"], value(lambda m: block_no(m) // 4 - 1))
                    nc.scalar.activation(prob[:, at, :], sc[k % 2][:], ACT.Exp, scale=SCALE).then_inc(s["exp_done"], 1)

                def copy_context(m, value, g, step):
                    if step != ph.steps - 1:
                        return
                    act.wait_ge(s["pv_done"], value(lambda m: (slot(m, g) + 1) * ph.steps))
                    if not isinstance(m, int) or slot(m, g) > 0:
                        act.wait_ge(ready["T"], value(lambda m: ph.use["x", m, g - 1] if g else ph.use["x", m - 1, 3]))
                    nc.scalar.copy(ctxS[:], ctxp[:]).then_inc(s["ctx_copied"], 1)

                def high_part(a, c):
                    def f(m, value, _):
                        wait_bank(act, value, f"{a}{c}")
                        if not isinstance(m, int) or m > 0:
                            act.wait_ge(d_write[c], value(lambda m: 144 * m))
                        nc.scalar.activation(part[a, c, 0][:], bank[ph.bank_of[f"{a}{c}"]][:], ACT.Identity,
                                             bias=bias_col[fam, a][:, c:c + 1]).then_inc(s["qk_high"], 1)
                    return f

                def copy_bank(kind, to):
                    def f(m, value, _):
                        wait_bank(act, value, kind)
                        if kind == "ct0" and (not isinstance(m, int) or m > 0):
                            act.wait_ge(ready[ph.bank_of["o1"]], value(lambda m: ph.use["o1", m - 1, 0]))
                        nc.scalar.copy(to, bank[ph.bank_of[kind]][:]).then_inc(free[ph.bank_of[kind]], 1)
                    return f

                ph.run(act, dict(s=exponent, pv=copy_context, q0=high_part("q", 0), k0=high_part("k", 0), q1=high_part("q", 1),
                                 k1=high_part("k", 1), t0=copy_bank("t0", hnT[:, 0, :]), t1=copy_bank("t1", hnT[:, 1, :]),
                                 ct0=copy_bank("ct0", ctxT[:, 0, :]), ct1=copy_bank("ct1", ctxT[:, 1, :])))

            piece = {"q0": 1, "k0": 2, "q1": 3, "k1": 4}

            @block.vector
            def _(dve):
                def linker(value, key):
                    done = [0]

                    def link(ins):
                        done[0] += 1
                        ins.then_inc(s["chain"], 1)
                        k = done[0]
                        hold(dve, s["chain"], value(lambda m: ph.chained[key[0], m, key[1]] + k))
                    return link, done

                def maximum(m, value, g, k):
                    t, j = divmod(k, 4)
                    block_no = lambda m: slot(m, g) * NB + k
                    if k == 0 and (not isinstance(m, int) or slot(m, g) > 0):
                        dve.wait_ge(s["max_split"], value(lambda m: slot(m, g)))
                    dve.wait_ge(s["max_ready"], value(lambda m: block_no(m) + 1))
                    if second:
                        ins = nc.vector.tensor_reduce(mf[:, t, j:j + 1], mx[k % 2][:], AX.X, ALU.max, negate=True)
                    else:
                        ins = nc.vector.tensor_reduce(mf[:, :, j], mx[k % 2][:].rearrange("p (i q) -> p i q", i=NT), AX.X, ALU.max, negate=True)
                    ins.then_inc(s["max_done"], 1)
                    if k == NB - 1:
                        link, done = linker(value, ("ms", g))
                        dve.wait_ge(s["max_done"], value(lambda m: block_no(m) + 1))
                        if not isinstance(m, int) or slot(m, g) > 0:
                            dve.wait_ge(ready["T"], value(lambda m: ph.use["m", m, g - 1] if g else ph.use["m", m - 1, 3]))
                        link(nc.vector.tensor_copy(mh[:, :, 0, :], mf[:]))
                        nc.vector.tensor_tensor(mh[:, :, 1, :], mf[:], mh[:, :, 0, :], ALU.subtract).then_inc(s["max_split"], 1)
                        assert done[0] == ph.chain["ms"]

                def max_rows(m, value, g):
                    wait_bank(dve, value, "m", g)
                    if not isinstance(m, int) or slot(m, g) > 0:
                        dve.wait_ge(d_max[(g - 1) % 4], value(lambda m: 32 * (m + 1 if g else m)))
                    nc.vector.tensor_copy(mrow[:], bank["T"][0:2 * GH, :].bitcast(BF16)[:, 0:TOK]).then_inc(free["T"], 1)

                def normalise(m, value, g):
                    link, done = linker(value, ("x", g))
                    wait_bank(dve, value, "x", g)
                    heads = bank["T"][:].rearrange("p (i j e) -> p i j e", i=NT, j=GH)
                    link(nc.vector.reciprocal(rden[:], heads[:, :, :, HD]))
                    if not isinstance(m, int) or m > 0:
                        dve.wait_ge(ready[ph.bank_of[f"ct{g // 2}"]], value(lambda m: ph.use[f"ct{g // 2}", m - 1, 0]))
                    to = ctxn[:, :, g * 64:(g + 1) * 64].rearrange("p i (j e) -> p i j e", j=GH)
                    for i in range(NT):
                        last = nc.vector.tensor_tensor(to[:, i], heads[:, i, :, 0:HD],
                                                       rden[:, i, :].unsqueeze(2).to_broadcast([P, GH, HD]), ALU.mult)
                    last.then_inc(free["T"], 1)

                def rest_part(a, c):
                    kind = f"{a}{c}"

                    def f(m, value, _):
                        dve.wait_ge(s["qk_high"], value(lambda m: 4 * m + piece[kind]))
                        if not isinstance(m, int) or c or m > 0:
                            dve.wait_ge(s["qk_parts"], value(lambda m: 4 * m + piece[kind] - 2))
                        nc.vector.scalar_tensor_tensor(out=rest[a][:], in0=bank[ph.bank_of[kind]][:], scalar=bias_col[fam, a][:, c:c + 1],
                                                       in1=part[a, c, 0][:], op0=ALU.add, op1=ALU.subtract).then_inc(free[ph.bank_of[kind]], 1)
                    return f

                def take_values(kind, half):
                    def f(m, value, _):
                        wait_bank(dve, value, kind)
                        if half == 0 and (not isinstance(m, int) or m > 0):
                            dve.wait_ge(s["v_copied"], value(lambda m: 4 * m))
                        nc.vector.tensor_tensor(vs[:, 2 * half:2 * half + 2, :], bank[ph.bank_of[kind]][:].rearrange("p (i o) -> p i o", i=2),
                                                bias_row[fam, "v"][:].unsqueeze(1).to_broadcast([P, 2, D]), ALU.add).then_inc(free[ph.bank_of[kind]], 1)
                    return f

                def add_residual(kind, half):
                    def f(m, value, _):
                        wait_bank(dve, value, kind)
                        if half == 0:
                            dve.wait_ge(s["res_ready"], value(lambda m: m + 1))
                            if not isinstance(m, int) or m > 0:
                                dve.wait_ge(d_out, value(lambda m: 16 * m))
                        nc.vector.tensor_tensor(hout[:, 2 * half:2 * half + 2, :], bank[ph.bank_of[kind]][:].rearrange("p (i o) -> p i o", i=2),
                                                res[:, 2 * half:2 * half + 2, :], ALU.add).then_inc(free[ph.bank_of[kind]], 1)
                    return f

                def experts(a):
                    kind = "w" + a

                    def f(m, value, _):
                        wait_bank(dve, value, kind)
                        nc.vector.tensor_tensor(W[a][:], bank[ph.bank_of[kind]][:].rearrange("p (c o) -> p c o", c=KC),
                                                main[a][:], ALU.add).then_inc(free[ph.bank_of[kind]], 1)
                    return f

                def layer_norm(kind, src, dst, done_sem):
                    def f(m, value, _):
                        link, done = linker(value, (kind, 0))
                        st, ag, rt = stats[kind], aggr[kind], root[kind]
                        if kind == "pn":
                            dve.wait_ge(s["pe_added"], value(lambda m: m + 1))
                        else:
                            dve.wait_ge(free[ph.bank_of["o1"]], value(use("o1")))
                            dve.wait_ge(free[ph.bank_of["o0"]], value(use("o0")))
                        for i in range(NT):
                            ins = nc.vector.bn_stats(st[:, i, :], src[:, i, :])
                        link(ins)
                        for i in range(NT):
                            ins = nc.vector.bn_aggr(ag[:, i, :], st[:, i, :])
                        link(ins)
                        var = rt[:, 3, :]
                        link(nc.vector.tensor_scalar(var, ag[:, :, 1], EPS, None, ALU.add))
                        rs = rt[:, 0, :]
                        link(rsqrt(nc.vector, link, rs, var, rt[:, 1, :], rt[:, 0, :].bitcast(I32), rt[:, 2, :]))
                        if kind == "pn":
                            if not isinstance(m, int) or m > 0:
                                dve.wait_ge(ready[ph.bank_of["t1"]], value(lambda m: ph.use["t1", m - 1, 0]))
                        elif not isinstance(m, int) or m > 0:
                            dve.wait_ge(d_out2, value(lambda m: 16 * m))
                            dve.wait_ge(ready[ph.bank_of["pl"]], value(lambda m: ph.use["pl", m - 1, 0]))
                        for i in range(NT):
                            ins = nc.vector.tensor_scalar(dst[:, i, :], src[:, i, :], ag[:, i, 0:1], rt[:, 0, i:i + 1], ALU.subtract, ALU.mult)
                        ins.then_inc(done_sem, 1)
                        assert done[0] == ph.chain[kind], done
                    return f

                def pool_tokens(m, value, _):
                    wait_bank(dve, value, "pl")
                    nc.vector.tensor_tensor(pooled[:].rearrange("p c b -> p (c b)"), bank[ph.bank_of["pl"]][:, 0:KC * BATCH],
                                            pooled[:].rearrange("p c b -> p (c b)"), ALU.add).then_inc(free[ph.bank_of["pl"]], 1)

                h = dict(M=maximum, m=max_rows, x=normalise, q0=rest_part("q", 0), k0=rest_part("k", 0), q1=rest_part("q", 1),
                         k1=rest_part("k", 1), v0=take_values("v0", 0), v1=take_values("v1", 1), o0=add_residual("o0", 0),
                         o1=add_residual("o1", 1), wq=experts("q"), wk=experts("k"), wv=experts("v"), wo=experts("o"), pl=pool_tokens,
                         ln=layer_norm("ln", hout, hnew, s["hnew_ready"]))
                if not second:
                    h["pn"] = layer_norm("pn", emb_t, xn, s["xn_ready"])
                ph.run(dve, h)

            @block.gpsimd
            def _(pool):
                def low_parts(a, c):
                    kind = f"{a}{c}"

                    def f(m, value, _):
                        hold(pool, free[ph.bank_of[kind]], value(use(kind)))
                        if not isinstance(m, int) or m > 0:
                            hold(pool, d_write[c], value(lambda m: 144 * m))
                        nc.gpsimd.tensor_copy(part[a, c, 1][:], rest[a][:]).then_inc(s["qk_rest"], 1)
                        hold(pool, s["qk_rest"], value(lambda m: 4 * m + piece[kind]))
                        nc.gpsimd.tensor_tensor(part[a, c, 2][:], rest[a][:], part[a, c, 1][:], ALU.subtract).then_inc(s["qk_parts"], 1)
                    return f

                def copy_values(m, value, g):
                    hold(pool, free[ph.bank_of["v1"]], value(use("v1")))
                    if not isinstance(m, int) or m > 0:
                        hold(pool, s["pv_done"], value(lambda m: (slot(m - 1, g) + 1) * ph.steps))
                    for i in range(NT):
                        ins = nc.gpsimd.tensor_copy(vp[:, i, g * GH:(g + 1) * GH, 0:HD],
                                                    vs[:, i, g * 64:(g + 1) * 64].rearrange("p (j e) -> p j e", j=GH))
                    ins.then_inc(s["v_copied"], 1)

                def residual_bias(m, value, _):
                    hold(pool, d_res, value(lambda m: 16 * (m + 1)))
                    nc.gpsimd.tensor_tensor(res[:], res[:], bias_row[fam, "o"][:].unsqueeze(1).to_broadcast([P, NT, D]), ALU.add).then_inc(s["res_ready"], 1)

                def scale_factor(a):
                    def f(m, value, _):
                        if value(lambda m: uc_count(m, a)) != 1 if isinstance(m, int) else True:
                            if not isinstance(m, int) or m > 0:
                                hold(pool, ready[ph.bank_of["w" + a]], value(lambda m: ph.use["w" + a, m - 1, 0]))
                        i = "qkvo".index(a)
                        nc.gpsimd.tensor_copy(coef_b[a][:], coef[:, bass.ds(m, 1), i:i + 1].rearrange("p b x -> p (b x)")).then_inc(s["coef_ready"], 1)
                        hold(pool, s["coef_ready"], value(lambda m: uc_count(m, a)))
                        nc.gpsimd.tensor_scalar(uc[a][:], uall[a][:], coef_b[a][:, 0:1], None, ALU.mult).then_inc(s["uc_ready"], 1)
                    return f

                def embed(m, value, _):
                    hold(pool, d_idx, value(lambda m: 16 * (m + 1)))
                    if not isinstance(m, int) or m > 0:
                        hold(pool, s["xn_ready"], value(lambda m: m))
                        hold(pool, d_h0, value(lambda m: 16 * m))
                    for i in range(NT):
                        pool.indirect_dma_start(out=emb_t[:, i, :], out_offset=None, in_=io["emb"],
                                                in_offset=bass.IndirectOffsetOnAxis(ap=idx_t[:, i:i + 1], axis=0)).then_inc(d_x, 16)

                def add_positions(m, value, _):
                    hold(pool, d_x, value(lambda m: 64 * (m + 1)))
                    hold(pool, d_pe, value(lambda m: 16 * (m + 1)))
                    nc.gpsimd.tensor_tensor(emb_t[:], emb_t[:], pe_t[:], ALU.add).then_inc(s["pe_added"], 1)

                h = dict(q0=low_parts("q", 0), k0=low_parts("k", 0), q1=low_parts("q", 1), k1=low_parts("k", 1), vc=copy_values,
                         rb=residual_bias)
                if second:
                    h |= {"w" + a: scale_factor(a) for a in "qkvo"}
                else:
                    h |= dict(pg=embed, pa=add_positions)
                ph.run(pool, h)

            @block.sync
            def _(sp):
                def write_stack(m, value, c):
                    hold(sp, s["qk_parts"], value(lambda m: 4 * m + 2 * c + 2))
                    if not isinstance(m, int) or m > 0:
                        for g in (2 * c, 2 * c + 1):
                            hold(sp, d_read[g], value(lambda m: 64 * m))
                    for i in range(3):
                        sp.dma_start(qs_dram[c, i * HD:(i + 1) * HD].rearrange("e h t -> h e t"), part["q", c, i][:]).then_inc(d_write[c], 16)
                    for r, i in enumerate(PARTS_K):
                        sp.dma_start(ks_dram[c, r * HD:(r + 1) * HD].rearrange("e h t -> h e t"), part["k", c, i][:]).then_inc(d_write[c], 16)

                def read_stack(m, value, g):
                    c, heads = g // 2, slice(4 * (g % 2), 4 * (g % 2) + 4)
                    hold(sp, d_write[c], value(lambda m: 144 * (m + 1)))
                    if not isinstance(m, int) or m > 0:
                        hold(sp, s["score_ready"], value(lambda m: (slot(m - 1, g) + 1) * NB))
                    sp.dma_start(kstack[0:SPLIT, g], ks_dram[c, :, heads, :]).then_inc(d_read[g], 16)
                    sp.dma_start(qstack[0:3 * HD, g], qs_dram[c, :, heads, :]).then_inc(d_read[g], 16)
                    sp.dma_start(qstack[3 * HD:5 * HD, g], qs_dram[c, 0:2 * HD, heads, :]).then_inc(d_read[g], 16)
                    sp.dma_start(qstack[5 * HD:6 * HD, g], qs_dram[c, 0:HD, heads, :]).then_inc(d_read[g], 16)

                def max_rows(m, value, g):
                    hold(sp, free["T"], value(use("m", g)))
                    for a in range(2):
                        sp.dma_start(qstack[MAX0 + a:MAX0 + a + 1, g], mrow[a * GH:(a + 1) * GH, :]).then_inc(d_max[g], 16)

                def load_residual(m, value, _):
                    if not isinstance(m, int) or m > 0:
                        hold(sp, free[ph.bank_of["o1"]], value(lambda m: ph.use["o1", m - 1, 0]))
                    if second:
                        src = by_batch(h1_dram)
                    else:
                        src = h0_dram
                        hold(sp, d_h0, value(lambda m: 16 * (m + 1)))
                    sp.dma_start(res[:], src[m]).then_inc(d_res, 16)

                def prepare(m, value, _):
                    if second:
                        if not isinstance(m, int) or m > 0:
                            hold(sp, ready[ph.bank_of["t1"]], value(lambda m: ph.use["t1", m - 1, 0]))
                        sp.dma_start(xn[:], by_batch(xn_dram)[m]).then_inc(d_x, 16)
                        return
                    if not isinstance(m, int) or m > 0:
                        hold(sp, d_x, value(lambda m: 64 * m))
                        hold(sp, s["pe_added"], value(lambda m: m))
                    sp.dma_start(idx_t[:], io["tokens"][m]).then_inc(d_idx, 16)
                    sp.dma_start(pe_t[:], io["c_pe"][m]).then_inc(d_pe, 16)

                def store_embedded(m, value, _):
                    hold(sp, s["pe_added"], value(lambda m: m + 1))
                    sp.dma_start(h0_dram[m], emb_t[:]).then_inc(d_h0, 16)

                def store(m, value, _):
                    hold(sp, free[ph.bank_of["o1"]], value(use("o1")))
                    hold(sp, free[ph.bank_of["o0"]], value(use("o0")))
                    if second:
                        sp.dma_start(out[m].rearrange("(i p) c -> p i c", p=P), hout[:]).then_inc(d_out, 16)
                    else:
                        sp.dma_start(by_item(h1_dram)[m], hout[:]).then_inc(d_out, 16)

                def store_normalised(m, value, _):
                        hold(sp, s["hnew_ready"], value(lambda m: m + 1))
                        sp.dma_start(by_item(xn_dram)[m], hnew[:]).then_inc(d_out2, 16)

                h = dict(sw=write_stack, sr=read_stack, m=max_rows, rs=load_residual, prep=prepare, st=store)
                if not second:
                    h |= dict(ps=store_embedded, s2=store_normalised)
                ph.run(sp, h)
                hold(sp, d_out, 16 * ITEMS)
                if not second:
                    hold(sp, d_out2, 16 * ITEMS)

    def gating():
        gw1 = sb("gw1", [P, KC, GATE_H], F32)
        gb1 = sb("gb1", [GATE_H, 1], F32)
        gw2 = sb("gw2", [GATE_H, EXPERTS], F32)
        gb2 = sb("gb2", [BATCH, EXPERTS], F32)
        number = sb("number", [BATCH, EXPERTS], F32)
        spread = sb("spread", [EXPERTS, P], F32)
        hid = sb("hid", [GATE_H, BATCH], F32)
        logit = sb("logit", [BATCH, EXPERTS], F32)
        top = sb("top", [BATCH, 8], F32)
        topi = sb("topi", [BATCH, 8], U32)
        topf = sb("topf", [BATCH, 8], F32)
        e2 = sb("e2", [BATCH, 4], F32)
        gate = sb("gate", [BATCH, 2, EXPERTS], F32)
        gateT = sb("gateT", [EXPERTS, BATCH], F32)
        s_l, s_p, s_v, s_a = sem("g_loads"), sem("g_products"), sem("g_vector"), sem("g_exp")
        with nc.Block() as block:
            @block.sync
            def _(sp):
                loads = [(gw1[:], io["g_w1T"].rearrange("(c p) g -> p c g", p=P)), (gb1[:], io["g_b1"]), (gw2[:], io["g_w2T"]),
                         (gb2[:], io["g_b2"].to_broadcast([BATCH, EXPERTS])), (number[:], io["c_number"]), (spread[:], io["c_spread"])]
                for to, of in loads:
                    sp.dma_start(to, of).then_inc(s_l, 16)
                gating.loads = 16 * len(loads)

            @block.tensor
            def _(pe):
                pe.wait_ge(s_l, gating.loads)
                for c in range(KC):
                    last = nc.tensor.matmul(sc[0][0:GATE_H, 0:BATCH], gw1[:, c, :], pooled[:, c, :], start=(c == 0), stop=(c == KC - 1))
                last.then_inc(s_p, 1)
                pe.wait_ge(s_v, 1)
                nc.tensor.matmul(sc[1][0:BATCH, 0:EXPERTS], hid[:], gw2[:], start=True, stop=True).then_inc(s_p, 1)
                pe.wait_ge(s_v, 12)
                nc.tensor.transpose(mx[0][0:EXPERTS, 0:BATCH], gate[:, 0, :], ident[0:BATCH, 0:BATCH]).then_inc(s_p, 1)
                pe.wait_ge(s_v, 13)
                nc.tensor.matmul(mx[1][:, 0:BATCH], spread[:], gateT[:], start=True, stop=True).then_inc(s_p, 1)

            @block.scalar
            def _(act):
                act.wait_ge(s_v, 4)
                nc.scalar.activation(e2[:, 1:2], e2[:, 0:1], ACT.Exp).then_inc(s_a, 1)

            @block.vector
            def _(dve):
                v = nc.vector
                links = [0]

                def link(ins):
                    links[0] += 1
                    ins.then_inc(s_v, 1)
                    dve.wait_ge(s_v, links[0])

                v.memset(qstack[MASK0:MAX0], 0.0)
                dve.wait_ge(s_l, gating.loads)
                dve.wait_ge(s_p, 1)
                link(v.tensor_scalar(hid[:], sc[0][0:GATE_H, 0:BATCH], gb1[:, 0:1], 0.0, ALU.add, ALU.max))
                dve.wait_ge(s_p, 2)
                link(v.tensor_tensor(logit[:], sc[1][0:BATCH, 0:EXPERTS], gb2[:], ALU.add))
                link(v.max(top[:], logit[:]))
                link(v.tensor_tensor(e2[:, 0:1], top[:, 1:2], top[:, 0:1], ALU.subtract))
                link(v.max_index(topi[:], top[:], logit[:]))
                link(v.tensor_copy(topf[:], topi[:]))
                dve.wait_ge(s_a, 1)
                link(v.tensor_scalar(e2[:, 2:3], e2[:, 1:2], 1.0, None, ALU.add))
                link(v.reciprocal(e2[:, 0:1], e2[:, 2:3]))
                link(v.tensor_tensor(e2[:, 1:2], e2[:, 1:2], e2[:, 0:1], ALU.mult))
                for i in range(2):
                    link(v.tensor_scalar(gate[:, i, :], number[:], topf[:, i:i + 1], e2[:, i:i + 1], ALU.is_equal, ALU.mult))
                link(v.tensor_tensor(gate[:, 0, :], gate[:, 0, :], gate[:, 1, :], ALU.add))
                dve.wait_ge(s_p, 3)
                link(v.tensor_copy(gateT[:], mx[0][0:EXPERTS, 0:BATCH]))
                dve.wait_ge(s_p, 4)
                for i in range(4):
                    link(v.tensor_scalar(coef[:, :, i], mx[1][:, 0:BATCH], sall[:, i:i + 1], None, ALU.mult))

    setup()
    attention(False)
    gating()
    attention(True)


def positions():
    pos = np.arange(SEQ, dtype=np.float32)[:, None]
    i = np.arange(D)
    denom = np.power(np.float32(10000.0), (2 * (i // 2)).astype(np.float32) / np.float32(D), dtype=np.float32)
    angle = (pos / denom).astype(np.float32)
    return np.where(i % 2 == 0, np.sin(angle), np.cos(angle)).astype(np.float32)


def kernel(**inputs):
    import concourse.bacc as _bacc
    from concourse.bass_utils import run_bass_kernel_spmd as _run

    a = {k: np.asarray(v) for k, v in inputs.items()}
    lay = {}
    lay["tokens"] = a["x"].T.reshape(ITEMS, NT, P).transpose(0, 2, 1)
    lay["emb"] = a["L0_tok_emb"]
    for p in "qv":
        lay[f"a_dir_{p}T"] = a[f"L0_attn_dir_{p}"].T
        lay[f"a_A_{p}"] = a[f"L0_attn_A_{p}"]
        lay[f"a_B_{p}T"] = a[f"L0_attn_B_{p}"].T
        lay[f"a_mag_{p}"] = a[f"L0_attn_mag_{p}"].reshape(1, 1)
        lay[f"a_b{p}"] = a[f"L0_attn_bias_{p}"]
    lay["a_k_wT"], lay["a_bk"] = a["L0_attn_k_w"].T, a["L0_attn_k_b"]
    lay["a_out_wT"], lay["a_bo"] = a["L0_attn_out_w"].T, a["L0_attn_out_b"]
    for p in "qkvo":
        lay[f"f_{p}WmT"] = a[f"L0_ffn_{p}Wm"].T
        lay[f"f_{p}V"] = a[f"L0_ffn_{p}V"].reshape(P, D)
        lay[f"f_{p}UT"] = a[f"L0_ffn_{p}U"].transpose(0, 2, 1).reshape(P, D)
        lay[f"f_{p}S"] = a[f"L0_ffn_{p}S"].reshape(P, 1)
        lay[f"f_b{p}"] = a[f"L0_ffn_{p}b"]
    lay["g_w1T"], lay["g_b1"] = a["L0_ffn_gw1"].T, a["L0_ffn_gb1"].reshape(GATE_H, 1)
    lay["g_w2T"], lay["g_b2"] = a["L0_ffn_gw2"].T, a["L0_ffn_gb2"].reshape(1, EXPERTS)
    lay["c_ident"] = np.eye(P, dtype=np.float32)
    lay["c_mean"] = np.tile(np.eye(BATCH, dtype=np.float32) / SEQ, (P // BATCH, 1))
    lay["c_pe"] = np.repeat(positions(), BATCH, axis=0).reshape(ITEMS, NT, P, D).transpose(0, 2, 1, 3)
    lay["c_number"] = np.tile(np.arange(EXPERTS, dtype=np.float32), (BATCH, 1))
    lay["c_spread"] = np.repeat(np.eye(EXPERTS, dtype=np.float32), RANK, axis=1)

    nc = _bacc.Bacc("TRN2", target_bir_lowering=False, num_devices=1)
    arrays, io = {}, {}
    for name, v in lay.items():
        v = np.ascontiguousarray(v)
        arrays[f"in_{name}"] = v
        io[name] = nc.dram_tensor(f"in_{name}", v.shape, mybir.dt.from_np(v.dtype), kind="ExternalInput").ap()
    out = nc.dram_tensor("out_0", (BATCH, SEQ, D), F32, kind="ExternalOutput").ap()
    with ExitStack() as ctx:
        tower(nc, ctx, io, out)
    r = _run(nc, [arrays], core_ids=[0])
    return r.results[0]["out_0"]
```

```python
from contextlib import ExitStack

import numpy as np
import concourse.bass as bass
from concourse import mybir

F32, BF16, I32, U32 = mybir.dt.float32, mybir.dt.bfloat16, mybir.dt.int32, mybir.dt.uint32
ALU, ACT, AX = mybir.AluOpType, mybir.ActivationFunctionType, mybir.AxisListType

P = 128
BATCH, SEQ, D = 16, 512, 256
HEADS, HD = 16, 16
EXPERTS, RANK, GATE_H = 8, 16, 64
DORA_R = 8
TOK = 512
NT = TOK // P
ITEMS = BATCH * SEQ // TOK
KC = D // P
GROUPS, GH = 4, 4
SPLIT = 96
MASK0, MAX0, KALL = 96, 104, 106
SCALE = HD ** -0.5
EPS = 1e-5
FAR = 2.0 ** 40
PARTS = dict(q=(0, 0, 0, 1, 1, 2), k=(2, 0, 1, 0, 1, 0))
ROOT_STEPS = 12
NPROB = 8


def have(m):
    return 0 <= m < ITEMS


def weave(a, b):
    keyed = [((i + 0.5) / len(x), j, i, tok) for j, x in enumerate((a, b)) for i, tok in enumerate(x)]
    return [tok for _, _, _, tok in sorted(keyed, key=lambda e: e[:3])]


class Phase:


    def __init__(self, second):
        self.second = second
        self.blocks = 16 if second else 4
        self.steps = self.blocks // 4
        self.bank_of = dict(x="T", m="T", q0="A", k0="B", ct1="A", o0="B", o1="A", wo="B", q1="A", k1="B",
                            ct0="B", v0="A", v1="B", t0="A", t1="B", wq="A", wk="B", wv="A", pl="B")
        self.chain = dict(ms=1, x=1) if second else dict(ms=1, x=1, pns=2, lns=2, nm=1)
        self.use, self.chained = {}, {}
        count = {"T": 0, "A": 0, "B": 0}
        links = 0
        for n in range(-1, ITEMS + 1):
            for tok in self.tokens(n):
                kind, m, x = tok
                if kind in self.bank_of:
                    count[self.bank_of[kind]] += 1
                    self.use[kind, m, x] = count[self.bank_of[kind]]
                if kind == "M" and x[1] == self.blocks - 1:
                    self.chained["ms", m, x[0]] = links
                    links += self.chain["ms"]
                elif kind in self.chain:
                    self.chained[kind, m, x] = links
                    links += self.chain[kind]

    def roots(self, n):
        return [] if self.second else [("nm", n, i) for i in range(ROOT_STEPS)]

    def first_work(self, n, g):
        items, late, roots = [], [], self.roots(n)
        if g == 0:
            if have(n + 1) and n >= 1:
                items.append(("sw", n + 1, 0))
            items.append(("vc", n, 3))
            if have(n + 2):
                items.append(("pns", n + 2, 0))
                late.append(("ps", n + 2, 0))
            if n >= 1:
                items += [("ct1", n - 1, 0), ("o0", n - 1, 0), ("o1", n - 1, 0)]
                late.append(("st", n - 1, 0))
        if g == 1:
            if have(n + 1):
                items += [("q1", n + 1, 0), ("k1", n + 1, 0), ("qm", n + 1, 1), ("km", n + 1, 1)]
            items = ([("lns", n - 1, 0)] if n >= 1 else []) + weave(items, roots[:4])
            if have(n + 3):
                late.append(("prep", n + 3, 0))
        if g == 2:
            if have(n + 1):
                items += [("sw", n + 1, 1), ("v0", n + 1, 0), ("v1", n + 1, 0)]
            items = weave(items, roots[4:]) + ([("pna", n + 2, 0)] if have(n + 2) else [])
            late += [("rs", n, 0), ("rb", n, 0)]
        if g == 3:
            if have(n + 3):
                items.append(("pg", n + 3, 0))
                late.append(("pa", n + 3, 0))
            items.append(("ct0", n, 0))
            if n >= 1:
                items.append(("lna", n - 1, 0))
            if have(n + 2):
                items += [("t0", n + 2, 0), ("t1", n + 2, 0)]
            if n >= 1:
                items.append(("pl", n - 1, 0))
                late.append(("s2", n - 1, 0))
            if have(n + 2):
                items += [(x, n + 2, 0) for x in ("q0", "k0", "qm", "km")]
            if have(n + 1):
                late += [("vc", n + 1, i) for i in range(3)]
        return items, late

    def second_work(self, n, g):
        items, late = [], []
        if g == 0:
            items.append(("vc", n, 3))
            if have(n + 1):
                items += [(x, n + 1, 0) for x in ("q0", "k0", "qm", "km")]
                late.append(("sw", n + 1, 0))
            if have(n + 2):
                items.insert(0, ("prep", n + 2, 0))
        if g == 1:
            if n >= 1:
                items += [("ct1", n - 1, 0), ("o0", n - 1, 0), ("o1", n - 1, 0)]
                late.append(("st", n - 1, 0))
            items.append(("wo", n, 0))
            if have(n + 1) and n >= 0:
                items.append(("wv", n + 1, 0))
        if g == 2:
            items.append(("rs", n, 0))
            if have(n + 1):
                items += [("q1", n + 1, 0), ("k1", n + 1, 0), ("qm", n + 1, 1), ("km", n + 1, 1)]
                late.append(("sw", n + 1, 1))
            late.append(("rb", n, 0))
        if g == 3:
            items.append(("ct0", n, 0))
            if have(n + 1):
                items += [("v0", n + 1, 0), ("v1", n + 1, 0)]
                late += [("vc", n + 1, i) for i in range(3)]
            if have(n + 2):
                items += [(x, n + 2, 0) for x in ("t0", "t1", "wq", "wk")]
        return items, late

    def tokens(self, n):
        if n == -1:
            prepare = lambda m: ([(x, m, 0) for x in ("prep", "pg", "pa", "ps", "pns")] + self.roots(m - 2)
                                 + [(x, m, 0) for x in ("pna", "t0", "t1")]
                                 + [(x, m, 0) for x in ("wq", "wk", "wv")[:3 - m] if self.second])
            half = lambda m, c: [(f"q{c}", m, 0), (f"k{c}", m, 0), ("qm", m, c), ("km", m, c), ("sw", m, c)]
            out = prepare(0) + half(0, 0) + half(0, 1) + [("sr", 0, 0), ("sr", 0, 1), ("v0", 0, 0), ("v1", 0, 0)]
            out += [("vc", 0, 0), ("vc", 0, 1), ("vc", 0, 2), ("sr", 0, 2)] + prepare(1)
            if not self.second:
                out += half(1, 0) + [("prep", 2, 0), ("pg", 2, 0), ("pa", 2, 0)]
            out += [("M", 0, (g, k)) for g in range(2) for k in range(self.blocks)]
            return out + [("m", 0, 0), ("md", 0, 0)]
        if n == ITEMS:
            out = [("pv", n - 1, (3, self.steps - 1)), ("x", n - 1, 3), ("ct1", n - 1, 0), ("o0", n - 1, 0), ("o1", n - 1, 0)]
            if not self.second:
                out += [("lns", n - 1, 0)] + self.roots(n) + [("lna", n - 1, 0), ("pl", n - 1, 0)]
            return out + [("st", n - 1, 0), ("s2", n - 1, 0)]
        out = []
        for g in range(GROUPS):
            ahead = lambda d: (n + (g + d) // 4, (g + d) % 4)
            before = (n, g - 1) if g else (n - 1, 3)
            started = [tok for tok in [("sr", *ahead(3)), ("md", *ahead(1))] if have(tok[1])]
            more, late = self.second_work(n, g) if self.second else self.first_work(n, g)
            turned = [("x", *before)] if have(before[0]) else []
            first = 1 if self.second or g in (0, 3) else 2
            items = started + more[:first] + turned + more[first:]
            done = 0
            for k in range(self.blocks):
                out.append(("s", n, (g, k)))
                if k % 4 == 1:
                    step = g * self.steps + k // 4 - 1
                    if step >= 0:
                        out.append(("pv", n, (step // self.steps, step % self.steps)))
                    elif n > 0:
                        out.append(("pv", n - 1, (3, self.steps - 1)))
                if have(ahead(2)[0]):
                    out.append(("M", ahead(2)[0], (ahead(2)[1], k)))
                if k == (1 if self.second else 0) and have(ahead(1)[0]):
                    out.append(("m", *ahead(1)))
                if k >= 1:
                    upto = (k * len(items)) // (self.blocks - 1)
                    out += items[done:upto]
                    done = upto
            out += late
        return out

    def run(self, engine, handlers):
        def emit(template, reg):
            for kind, m, x in self.tokens(template):
                if kind not in handlers:
                    continue
                if reg is None:
                    value = lambda f, m=m: f(m)
                    item = m
                else:
                    def value(f, m=m):
                        a, b = f(m), f(m + 1)
                        assert a > 0 and f(m + ITEMS - 6) == a + (b - a) * (ITEMS - 6), kind
                        return reg * (b - a) + (a - 2 * (b - a)) if b != a else a
                    item = reg + (m - 2) if m != 2 else reg
                if isinstance(x, tuple):
                    handlers[kind](item, value, *x)
                else:
                    handlers[kind](item, value, x)
        emit(-1, None)
        emit(0, None)
        emit(1, None)
        with engine.Fori(2, ITEMS - 3) as n:
            emit(2, n)
        for n in range(ITEMS - 3, ITEMS + 1):
            emit(n, None)


def tower(nc, ctx, io, out):
    sb = lambda name, shape, dt: ctx.enter_context(nc.sbuf_tensor(name, shape, dt))
    ps = lambda name: ctx.enter_context(nc.psum_tensor(name, [P, 512], F32))
    sem = lambda name: ctx.enter_context(nc.semaphore(name))
    dram = lambda name, shape, dt: nc.dram_tensor(name, shape, dt, kind="Internal").ap()

    h0_dram = dram("h0_rows", [ITEMS, P, NT, D], F32)
    h1_dram = dram("h1_rows", [SEQ * BATCH, D], F32)
    xn_dram = dram("xn_rows", [SEQ * BATCH, D], F32)
    stack_dram = {a: dram(f"{a}_stack", [2, P, SPLIT // HD, TOK], BF16) for a in "qk"}
    by_batch = lambda t: t.rearrange("(i p b) c -> b p i c", p=P, b=BATCH)
    by_item = lambda t: t.rearrange("(n i p) c -> n p i c", p=P, i=NT)

    qstack = sb("qstack", [P, GROUPS, GH, TOK], BF16)
    kstack = sb("kstack", [P, GROUPS, GH, TOK], BF16)
    prob = sb("prob", [P, NPROB, TOK], F32)
    vp = sb("vp", [P, NT, HEADS, 32], F32)
    vs = sb("vs", [P, NT, D], F32)
    xn = sb("xn", [P, NT, D], F32)
    hnT = sb("hnT", [P, KC, TOK], F32)
    ctxS = sb("ctxS", [P, TOK], F32)
    ctxn = sb("ctxn", [P, NT, D], F32)
    ctxT = sb("ctxT", [P, KC, TOK], F32)
    res = sb("res", [P, NT, D], F32)
    hout = sb("hout", [P, NT, D], F32)
    hnew = sb("hnew", [P, NT, D], F32)
    part = {(a, c, i): sb(f"part_{a}{c}{i}", [P, TOK], BF16) for a in "qk" for c in range(2) for i in range(3)}
    rest = {a: sb(f"rest_{a}", [P, TOK], F32) for a in "qk"}
    W = {a: sb(f"w_{a}", [P, KC, D], F32) for a in "qkvo"}
    mf = sb("mf", [P, NT, GH], F32)
    mh = sb("mh", [P, NT, 2, GH], BF16)
    mrow = sb("mrow", [2 * GH, TOK], BF16)
    rden = sb("rden", [P, NT, GH], F32)
    emb_t = sb("emb_t", [P, NT, D], F32)
    pe_t = sb("pe_t", [P, NT, D], F32)
    idx_t = sb("idx_t", [P, NT], I32)
    stats = {a: sb(f"stats_{a}", [P, NT, 6], F32) for a in ("pn", "ln")}
    aggr = sb("aggr", [P, 2 * NT, 2], F32)
    root = sb("root", [P, 4, 2 * NT], F32)
    ident = sb("ident", [P, P], F32)
    identb = sb("identb", [P, P], BF16)
    ones = sb("ones", [P, P], F32)
    mean_sel = sb("mean_sel", [P, BATCH], F32)
    pooled = sb("pooled", [P, KC, BATCH], F32)
    bias_col = {(f, a): sb(f"bias_{f}{a}", [P, KC], F32) for f in "af" for a in "qk"}
    bias_row = {(f, a): sb(f"bias_{f}{a}", [P, D], F32) for f in "af" for a in "vo"}
    main = {a: sb(f"main_{a}", [P, KC, D], F32) for a in "qkvo"}
    vall = {a: sb(f"vall_{a}", [P, D], F32) for a in "qkvo"}
    uall = {a: sb(f"uall_{a}", [P, D], F32) for a in "qkvo"}
    uc = {a: sb(f"uc_{a}", [P, D], F32) for a in "qkvo"}
    sall = sb("sall", [P, 4], F32)
    coef = sb("coef", [P, BATCH, 4], F32)
    coef_b = {a: sb(f"coef_{a}", [P, 1], F32) for a in "qkvo"}

    sc = [ps("sc0"), ps("sc1")]
    mx = [ps("mx0"), ps("mx1")]
    ctxp = ps("ctxp")
    bank = {"T": ps("bankT"), "A": ps("bankA"), "B": ps("bankB")}

    def rsqrt_steps(eng, dst, var, tmp, y):
        magic = tmp.bitcast(I32)
        steps = [lambda: eng.tensor_scalar(magic, var.bitcast(I32), 1, None, ALU.logical_shift_right),
                 lambda: eng.tensor_scalar(y.bitcast(I32), magic, -1.0, float(0x5F3759DF), ALU.mult, ALU.add)]
        for i in range(3):
            to = dst if i == 2 else y
            steps += [lambda: eng.tensor_tensor(tmp, y, y, ALU.mult),
                      lambda: eng.scalar_tensor_tensor(out=tmp, in0=tmp, scalar=-0.5, in1=var, op0=ALU.mult, op1=ALU.mult),
                      lambda to=to: eng.scalar_tensor_tensor(out=to, in0=tmp, scalar=1.5, in1=y, op0=ALU.add, op1=ALU.mult)]
        return steps

    s_late = sem("su_late_loads")

    def setup():
        A_t = {a: sb(f"dora_a_{a}", [DORA_R, D], F32) for a in "qv"}
        Bt_t = {a: sb(f"dora_b_{a}", [DORA_R, D], F32) for a in "qv"}
        mag = sb("mag", [P, 2], F32)
        sq = sb("sq", [P, 2, D * KC], F32)
        ssum = sb("ssum", [P, 2], F32)
        tot = sb("tot", [P, 2], F32)
        tmp3 = sb("tmp3", [P, 3, 2], F32)
        mask_f = sb("mask_f", [MAX0 - MASK0, 2, TOK], F32)
        mask_b = sb("mask_b", [MAX0 - MASK0, 2, TOK], BF16)
        s_w, s_set, s_pe, s_chain = sem("su_loads"), sem("su_sums"), sem("su_products"), sem("su_chain")
        s_mask, s_fill, s_rows = sem("su_mask"), sem("su_fill"), sem("su_mask_rows")
        with nc.Block() as block:
            @block.sync
            def _(sp):
                half = lambda w: w.rearrange("(c p) o -> p c o", p=P)
                loads = [(ident[:], io["c_ident"]), (mask_f[:], io["c_mask"])]
                for i, a in enumerate("qv"):
                    loads += [(A_t[a][:], io[f"a_A_{a}"]), (Bt_t[a][:], io[f"a_B_{a}T"]), (W[a][:], half(io[f"a_dir_{a}T"]))]
                    loads.append((mag[:, i:i + 1], io[f"a_mag_{a}"].to_broadcast([P, 1])))
                loads += [(W["k"][:], half(io["a_k_wT"])), (W["o"][:], half(io["a_out_wT"])), (mean_sel[:], io["c_mean"])]
                later = []
                for f, to in (("a", loads), ("f", later)):
                    for a in "qk":
                        to.append((bias_col[f, a][:], io[f"{f}_b{a}"].rearrange("(c p) -> p c", p=P)))
                    for a in "vo":
                        to.append((bias_row[f, a][:], io[f"{f}_b{a}"].rearrange("(a c) -> a c", a=1).to_broadcast([P, D])))
                for i, a in enumerate("qkvo"):
                    later += [(main[a][:], half(io[f"f_{a}WmT"])), (vall[a][:], io[f"f_{a}V"]), (uall[a][:], io[f"f_{a}UT"])]
                    later.append((sall[:, i:i + 1], io[f"f_{a}S"]))
                with nc.allow_non_contiguous_dma(reason="a few hundred bytes of biases"):
                    for to, of in loads:
                        sp.dma_start(to, of).then_inc(s_w, 16)
                    for i, stack in enumerate((qstack, kstack)):
                        sp.wait_ge(s_mask, i + 1)
                        if i:
                            sp.wait_ge(s_fill, 1)
                        sp.dma_start(stack[MASK0:MAX0].rearrange("r g j t -> r (g j) t"),
                                     mask_b[:, i, :].unsqueeze(1).to_broadcast([MAX0 - MASK0, GROUPS * GH, TOK])).then_inc(s_rows, 16)
                    for to, of in later:
                        sp.dma_start(to, of).then_inc(s_late, 16)
                    sp.wait_ge(s_rows, 32)
                setup.loads = 16 * len(loads)
                setup.later = 16 * len(later)

            @block.gpsimd
            def _(pool):
                nc.gpsimd.memset(kstack[MASK0:P], 1.0).then_inc(s_fill, 1)

            @block.vector
            def _(dve):
                links = [0]

                def link(ins):
                    links[0] += 1
                    ins.then_inc(s_chain, 1)
                    dve.wait_ge(s_chain, links[0])

                link(nc.vector.memset(vp[:], 0.0))
                link(nc.vector.memset(vp[:, :, :, HD:HD + 1], 1.0))
                link(nc.vector.memset(ones[:], 1.0))
                link(nc.vector.memset(pooled[:], 0.0))
                link(nc.vector.memset(aggr[:], 1.0))
                dve.wait_ge(s_w, setup.loads)
                link(nc.vector.tensor_copy(identb[:], ident[:]))
                for i in range(2):
                    nc.vector.tensor_copy(mask_b[:, i, :], mask_f[:, i, :]).then_inc(s_mask, 1)
                for i, a in enumerate("qv"):
                    for c in range(KC):
                        dve.wait_ge(s_pe, 1)
                        link(nc.vector.tensor_tensor(W[a][:, c, :], sc[i][:, c * D:(c + 1) * D], W[a][:, c, :], ALU.add))
                    flat = W[a][:].rearrange("p c o -> p (c o)")
                    link(nc.vector.tensor_tensor(sq[:, i, :], flat, flat, ALU.mult))
                    nc.vector.tensor_reduce(ssum[:, i:i + 1], sq[:, i, :], AX.X, ALU.add).then_inc(s_set, 1)
                dve.wait_ge(s_pe, 2)
                link(nc.vector.tensor_copy(tot[:], mx[0][:, 0:2]))
                for step in rsqrt_steps(nc.vector, tmp3[:, 2, :], tot[:], tmp3[:, 0, :], tmp3[:, 1, :]):
                    link(step())
                link(nc.vector.tensor_tensor(tot[:], tot[:], tmp3[:, 2, :], ALU.mult))
                link(nc.vector.tensor_scalar(tot[:], tot[:], 1e-8, None, ALU.add))
                link(nc.vector.reciprocal(tmp3[:, 0, :], tot[:]))
                link(nc.vector.tensor_tensor(tot[:], tmp3[:, 0, :], mag[:], ALU.mult))
                for i, a in enumerate("qv"):
                    link(nc.vector.tensor_scalar(W[a][:], W[a][:], tot[:, i:i + 1], None, ALU.mult))

            @block.tensor
            def _(pe):
                pe.wait_ge(s_w, setup.loads)
                for i, a in enumerate("qv"):
                    for c in range(KC):
                        last = nc.tensor.matmul(sc[i][:, c * D:(c + 1) * D], A_t[a][:, c * P:(c + 1) * P], Bt_t[a][:],
                                                start=True, stop=True)
                last.then_inc(s_pe, 1)
                pe.wait_ge(s_set, 2)
                nc.tensor.matmul(mx[0][:, 0:2], ones[:], ssum[:], start=True, stop=True).then_inc(s_pe, 1)

    def attention(second):
        ph = Phase(second)
        NB = ph.blocks
        pre = "f_" if second else "a_"
        fam = "f" if second else "a"
        s = {x: sem(pre + x) for x in (
            "score_ready", "exp_done", "max_ready", "max_done", "max_split", "pv_done", "ctx_copied",
            "qk_high", "qk_rest", "qk_parts", "v_copied", "chain", "xn_ready", "res_ready", "hout_ready",
            "hnew_ready", "uc_ready", "coef_ready", "waits_done", "pe_added")}
        free = {b: sem(f"{pre}bank{b}_free") for b in bank}
        ready = {b: sem(f"{pre}bank{b}_ready") for b in bank}
        d_write = [sem(f"{pre}d_stack_write{c}") for c in range(2)]
        d_read = [sem(f"{pre}d_stack_read{g}") for g in range(GROUPS)]
        d_max = [sem(f"{pre}d_max_rows{g}") for g in range(GROUPS)]
        d_res, d_x, d_idx, d_pe, d_h0, d_out, d_out2 = (sem(pre + x) for x in (
            "d_res", "d_x", "d_idx", "d_pe", "d_h0", "d_out", "d_out2"))
        slot = lambda m, g: 4 * m + g
        use = lambda kind, x=0: (lambda m: ph.use[kind, m, x])

        uc_order = [(kind[1], m) for n in range(-1, ITEMS + 1) for kind, m, _ in ph.tokens(n) if kind in ("wq", "wk", "wv", "wo")]
        uc_count = lambda m, a: uc_order.index((a, m)) + 1

        def hold(eng, semaphore, count):
            eng.wait_ge(semaphore, count)
            if not isinstance(count, int):
                eng.sem_inc(s["waits_done"])

        def before_use(eng, value, kind, x=0):
            first = value(lambda m: ph.use[kind, m, x] - 1)
            if not (isinstance(first, int) and first == 0):
                eng.wait_ge(free[ph.bank_of[kind]], value(lambda m: ph.use[kind, m, x] - 1))

        def wait_bank(eng, value, kind, x=0):
            eng.wait_ge(ready[ph.bank_of[kind]], value(use(kind, x)))

        with nc.Block() as block:
            @block.tensor
            def _(pe):
                mm = nc.tensor.matmul

                def read_out(value, kind, *operands):
                    for x in operands:
                        if ph.bank_of[x] != ph.bank_of[kind]:
                            pe.wait_ge(free[ph.bank_of[x]], value(use(x)))

                def score(m, value, g, k):
                    t, j = divmod(k, 4)
                    if k == 0:
                        pe.wait_ge(d_read[g], value(lambda m: 32 * (m + 1)))
                        pe.wait_ge(d_max[g], value(lambda m: 32 * (m + 1)))
                    block_no = lambda m: slot(m, g) * NB + k
                    if value(block_no) not in (0, 1) if isinstance(m, int) else True:
                        pe.wait_ge(s["exp_done"], value(lambda m: block_no(m) - 1))
                    to = sc[k % 2]
                    if second:
                        last = mm(to[:], kstack[0:KALL, g, j, t * P:(t + 1) * P], qstack[0:KALL, g, j, :], start=True, stop=True)
                    else:
                        for i in range(NT):
                            cols = slice(i * P, (i + 1) * P)
                            last = mm(to[:, cols], kstack[0:KALL, g, j, cols], qstack[0:KALL, g, j, cols], start=True, stop=True)
                    last.then_inc(s["score_ready"], 1)

                def maximum(m, value, g, k):
                    t, j = divmod(k, 4)
                    if k == 0:
                        pe.wait_ge(d_read[g], value(lambda m: 32 * (m + 1)))
                    block_no = lambda m: slot(m, g) * NB + k
                    if not isinstance(m, int) or block_no(m) > 1:
                        pe.wait_ge(s["max_done"], value(lambda m: block_no(m) - 1))
                    to = mx[k % 2]
                    if second:
                        last = mm(to[:], qstack[0:MAX0, g, j, t * P:(t + 1) * P], kstack[0:MAX0, g, j, :], start=True, stop=True)
                    else:
                        for i in range(NT):
                            cols = slice(i * P, (i + 1) * P)
                            last = mm(to[:, cols], qstack[0:MAX0, g, j, cols], kstack[0:MAX0, g, j, cols], start=True, stop=True)
                    last.then_inc(s["max_ready"], 1)

                def values(m, value, g, step):
                    first = lambda m: (slot(m, g) * ph.steps + step) * 4
                    pe.wait_ge(s["exp_done"], value(lambda m: first(m) + 4))
                    if step == 0:
                        pe.wait_ge(s["v_copied"], value(lambda m: slot(m, g) + 1))
                        if not isinstance(m, int) or slot(m, g) > 0:
                            pe.wait_ge(s["ctx_copied"], value(lambda m: slot(m, g)))
                    at = (g * ph.steps + step) * 4 % NPROB
                    for i in range(1 if second else NT):
                        for j in range(GH):
                            h, cols = g * GH + j, slice(i * P, (i + 1) * P)
                            if second:
                                last = mm(ctxp[32 * j:32 * j + 32, :], vp[:, step, h, :], prob[:, at + j, :],
                                          start=(step == 0), stop=(step == ph.steps - 1))
                            else:
                                last = mm(ctxp[32 * j:32 * j + 32, cols], vp[:, i, h, :], prob[:, at + j, cols],
                                          start=True, stop=True)
                    last.then_inc(s["pv_done"], 1)

                def max_rows(m, value, g):
                    before_use(pe, value, "m", g)
                    pe.wait_ge(s["max_split"], value(lambda m: slot(m, g) + 1))
                    rows = bank["T"][0:2 * GH, :].bitcast(BF16)
                    for i in range(NT):
                        last = nc.tensor.transpose(rows[:, i * P:(i + 1) * P], mh[:, i, :, :].rearrange("p a j -> p (a j)"), identb[:])
                    last.then_inc(ready["T"], 1)

                def turn_context(m, value, g):
                    before_use(pe, value, "x", g)
                    pe.wait_ge(s["ctx_copied"], value(lambda m: slot(m, g) + 1))
                    for i in range(NT):
                        last = nc.tensor.transpose(bank["T"][:, i * P:(i + 1) * P], ctxS[:, i * P:(i + 1) * P], ident[:])
                    last.then_inc(ready["T"], 1)

                def turn_normal(c):
                    def f(m, value, _):
                        before_use(pe, value, f"ct{c}")
                        pe.wait_ge(free["T"], value(use("x", 2 * c + 1)))
                        to = bank[ph.bank_of[f"ct{c}"]]
                        for i in range(NT):
                            last = nc.tensor.transpose(to[:, i * P:(i + 1) * P], ctxn[:, i, c * P:(c + 1) * P], ident[:])
                        last.then_inc(ready[ph.bank_of[f"ct{c}"]], 1)
                    return f

                def turn_tokens(c):
                    def f(m, value, _):
                        before_use(pe, value, f"t{c}")
                        if second:
                            pe.wait_ge(d_x, value(lambda m: 16 * (m + 1)))
                        else:
                            pe.wait_ge(s["xn_ready"], value(lambda m: m + 1))
                        to = bank[ph.bank_of[f"t{c}"]]
                        for i in range(NT):
                            last = nc.tensor.transpose(to[:, i * P:(i + 1) * P], xn[:, i, c * P:(c + 1) * P], ident[:])
                        last.then_inc(ready[ph.bank_of[f"t{c}"]], 1)
                    return f

                def project_t(a, c):
                    def f(m, value, _):
                        before_use(pe, value, f"{a}{c}")
                        if c == 0:
                            read_out(value, f"{a}{c}", "t0", "t1", *(["w" + a] if second else []))
                        to = bank[ph.bank_of[f"{a}{c}"]]
                        for kc in range(KC):
                            last = mm(to[:], W[a][:, kc, c * P:(c + 1) * P], hnT[:, kc, :], start=(kc == 0), stop=(kc == KC - 1))
                        last.then_inc(ready[ph.bank_of[f"{a}{c}"]], 1)
                    return f

                def project(kind, a, half, src):
                    def f(m, value, _):
                        before_use(pe, value, kind)
                        if kind == "v0" and second:
                            read_out(value, kind, "wv")
                        if kind == "o0":
                            read_out(value, kind, "ct0", "ct1", *(["wo"] if second else []))
                        to = bank[ph.bank_of[kind]]
                        for i in (2 * half, 2 * half + 1):
                            for kc in range(KC):
                                last = mm(to[:, (i % 2) * D:(i % 2 + 1) * D], src[:, kc, i * P:(i + 1) * P], W[a][:, kc, :],
                                          start=(kc == 0), stop=(kc == KC - 1))
                        last.then_inc(ready[ph.bank_of[kind]], 1)
                    return f

                def experts(a):
                    def f(m, value, _):
                        before_use(pe, value, "w" + a)
                        pe.wait_ge(s["uc_ready"], value(lambda m: uc_count(m, a)))
                        to = bank[ph.bank_of["w" + a]]
                        for c in range(KC):
                            last = mm(to[:, c * D:(c + 1) * D], vall[a][:, c * P:(c + 1) * P], uc[a][:], start=True, stop=True)
                        last.then_inc(ready[ph.bank_of["w" + a]], 1)
                    return f

                def pool_tokens(m, value, _):
                    before_use(pe, value, "pl")
                    pe.wait_ge(s["hnew_ready"], value(lambda m: m + 1))
                    to = bank[ph.bank_of["pl"]]
                    for c in range(KC):
                        for i in range(NT):
                            last = mm(to[:, c * BATCH:(c + 1) * BATCH], hnew[:, i, c * P:(c + 1) * P], mean_sel[:],
                                      start=(i == 0), stop=(i == NT - 1))
                    last.then_inc(ready[ph.bank_of["pl"]], 1)

                ph.run(pe, dict(s=score, M=maximum, pv=values, m=max_rows, x=turn_context, ct0=turn_normal(0), ct1=turn_normal(1),
                                t0=turn_tokens(0), t1=turn_tokens(1), q0=project_t("q", 0), k0=project_t("k", 0),
                                q1=project_t("q", 1), k1=project_t("k", 1), v0=project("v0", "v", 0, hnT), v1=project("v1", "v", 1, hnT),
                                o0=project("o0", "o", 0, ctxT), o1=project("o1", "o", 1, ctxT), wq=experts("q"), wk=experts("k"),
                                wv=experts("v"), wo=experts("o"), pl=pool_tokens))

            @block.scalar
            def _(act):
                def exponent(m, value, g, k):
                    block_no = lambda m: slot(m, g) * NB + k
                    at = (g * NB + k) % NPROB
                    act.wait_ge(s["score_ready"], value(lambda m: block_no(m) + 1))
                    if k % 4 == 0 and (not isinstance(m, int) or block_no(m) >= NPROB):
                        act.wait_ge(s["pv_done"], value(lambda m: block_no(m) // 4 - 1))
                    nc.scalar.activation(prob[:, at, :], sc[k % 2][:], ACT.Exp, scale=SCALE).then_inc(s["exp_done"], 1)

                def copy_context(m, value, g, step):
                    if step != ph.steps - 1:
                        return
                    act.wait_ge(s["pv_done"], value(lambda m: (slot(m, g) + 1) * ph.steps))
                    if not isinstance(m, int) or slot(m, g) > 0:
                        act.wait_ge(ready["T"], value(lambda m: ph.use["x", m, g - 1] if g else ph.use["x", m - 1, 3]))
                    nc.scalar.copy(ctxS[:], ctxp[:]).then_inc(s["ctx_copied"], 1)

                def high_part(a, c):
                    def f(m, value, _):
                        wait_bank(act, value, f"{a}{c}")
                        if not isinstance(m, int) or m > 0:
                            act.wait_ge(d_write[c], value(lambda m: 96 * m))
                        nc.scalar.activation(part[a, c, 0][:], bank[ph.bank_of[f"{a}{c}"]][:], ACT.Identity,
                                             bias=bias_col[fam, a][:, c:c + 1]).then_inc(s["qk_high"], 1)
                    return f

                def max_rows(m, value, g):
                    hold(act, free["T"], value(use("m", g)))
                    for a in range(2):
                        act.dma_start(qstack[MAX0 + a:MAX0 + a + 1, g], mrow[a * GH:(a + 1) * GH, :]).then_inc(d_max[g], 16)

                def middle_part(a):
                    def f(m, value, c):
                        act.wait_ge(free[ph.bank_of[f"{a}{c}"]], value(use(f"{a}{c}")))
                        nc.scalar.copy(part[a, c, 1][:], rest[a][:]).then_inc(s["qk_rest"], 1)
                    return f

                def copy_bank(kind, to):
                    def f(m, value, _):
                        wait_bank(act, value, kind)
                        if kind == "ct0" and (not isinstance(m, int) or m > 0):
                            act.wait_ge(ready[ph.bank_of["o1"]], value(lambda m: ph.use["o1", m - 1, 0]))
                        nc.scalar.copy(to, bank[ph.bank_of[kind]][:]).then_inc(free[ph.bank_of[kind]], 1)
                    return f

                ph.run(act, dict(s=exponent, md=max_rows, pv=copy_context, q0=high_part("q", 0), k0=high_part("k", 0), q1=high_part("q", 1),
                                 k1=high_part("k", 1), qm=middle_part("q"), km=middle_part("k"), t0=copy_bank("t0", hnT[:, 0, :]), t1=copy_bank("t1", hnT[:, 1, :]),
                                 ct0=copy_bank("ct0", ctxT[:, 0, :]), ct1=copy_bank("ct1", ctxT[:, 1, :])))

            piece = {"q0": 1, "k0": 2, "q1": 3, "k1": 4}

            @block.vector
            def _(dve):
                def linker(value, key):
                    done = [0]

                    def link(ins):
                        done[0] += 1
                        ins.then_inc(s["chain"], 1)
                        k = done[0]
                        hold(dve, s["chain"], value(lambda m: ph.chained[key[0], m, key[1]] + k))
                    return link, done

                def maximum(m, value, g, k):
                    t, j = divmod(k, 4)
                    block_no = lambda m: slot(m, g) * NB + k
                    if k == 0 and (not isinstance(m, int) or slot(m, g) > 0):
                        dve.wait_ge(s["max_split"], value(lambda m: slot(m, g)))
                    dve.wait_ge(s["max_ready"], value(lambda m: block_no(m) + 1))
                    if second:
                        ins = nc.vector.tensor_reduce(mf[:, t, j:j + 1], mx[k % 2][:], AX.X, ALU.max, negate=True)
                    else:
                        ins = nc.vector.tensor_reduce(mf[:, :, j], mx[k % 2][:].rearrange("p (i q) -> p i q", i=NT), AX.X, ALU.max, negate=True)
                    ins.then_inc(s["max_done"], 1)
                    if k == NB - 1:
                        link, done = linker(value, ("ms", g))
                        dve.wait_ge(s["max_done"], value(lambda m: block_no(m) + 1))
                        if not isinstance(m, int) or slot(m, g) > 0:
                            dve.wait_ge(ready["T"], value(lambda m: ph.use["m", m, g - 1] if g else ph.use["m", m - 1, 3]))
                        link(nc.vector.tensor_copy(mh[:, :, 0, :], mf[:]))
                        nc.vector.tensor_tensor(mh[:, :, 1, :], mf[:], mh[:, :, 0, :], ALU.subtract).then_inc(s["max_split"], 1)
                        assert done[0] == ph.chain["ms"]

                def max_rows(m, value, g):
                    wait_bank(dve, value, "m", g)
                    if not isinstance(m, int) or slot(m, g) > 0:
                        dve.wait_ge(d_max[(g - 1) % 4], value(lambda m: 32 * (m + 1 if g else m)))
                    nc.vector.tensor_copy(mrow[:], bank["T"][0:2 * GH, :].bitcast(BF16)[:, 0:TOK]).then_inc(free["T"], 1)

                def normalise(m, value, g):
                    link, done = linker(value, ("x", g))
                    wait_bank(dve, value, "x", g)
                    heads = bank["T"][:].rearrange("p (i j e) -> p i j e", i=NT, j=GH)
                    link(nc.vector.reciprocal(rden[:], heads[:, :, :, HD]))
                    if not isinstance(m, int) or m > 0:
                        dve.wait_ge(ready[ph.bank_of[f"ct{g // 2}"]], value(lambda m: ph.use[f"ct{g // 2}", m - 1, 0]))
                    to = ctxn[:, :, g * 64:(g + 1) * 64].rearrange("p i (j e) -> p i j e", j=GH)
                    for i in range(NT):
                        last = nc.vector.tensor_tensor(to[:, i], heads[:, i, :, 0:HD],
                                                       rden[:, i, :].unsqueeze(2).to_broadcast([P, GH, HD]), ALU.mult)
                    last.then_inc(free["T"], 1)

                def rest_part(a, c):
                    kind = f"{a}{c}"

                    def f(m, value, _):
                        dve.wait_ge(s["qk_high"], value(lambda m: 4 * m + piece[kind]))
                        if not isinstance(m, int) or c or m > 0:
                            dve.wait_ge(s["qk_parts"], value(lambda m: 4 * m + piece[kind] - 2))
                        nc.vector.scalar_tensor_tensor(out=rest[a][:], in0=bank[ph.bank_of[kind]][:], scalar=bias_col[fam, a][:, c:c + 1],
                                                       in1=part[a, c, 0][:], op0=ALU.add, op1=ALU.subtract).then_inc(free[ph.bank_of[kind]], 1)
                    return f

                def take_values(kind, half):
                    def f(m, value, _):
                        wait_bank(dve, value, kind)
                        if half == 0 and (not isinstance(m, int) or m > 0):
                            dve.wait_ge(s["v_copied"], value(lambda m: 4 * m))
                        nc.vector.tensor_tensor(vs[:, 2 * half:2 * half + 2, :], bank[ph.bank_of[kind]][:].rearrange("p (i o) -> p i o", i=2),
                                                bias_row[fam, "v"][:].unsqueeze(1).to_broadcast([P, 2, D]), ALU.add).then_inc(free[ph.bank_of[kind]], 1)
                    return f

                def add_residual(kind, half):
                    def f(m, value, _):
                        wait_bank(dve, value, kind)
                        if half == 0:
                            dve.wait_ge(s["res_ready"], value(lambda m: m + 1))
                            if not isinstance(m, int) or m > 0:
                                dve.wait_ge(d_out, value(lambda m: 16 * m))
                        nc.vector.tensor_tensor(hout[:, 2 * half:2 * half + 2, :], bank[ph.bank_of[kind]][:].rearrange("p (i o) -> p i o", i=2),
                                                res[:, 2 * half:2 * half + 2, :], ALU.add).then_inc(free[ph.bank_of[kind]], 1)
                    return f

                def experts(a):
                    kind = "w" + a

                    def f(m, value, _):
                        wait_bank(dve, value, kind)
                        nc.vector.tensor_tensor(W[a][:], bank[ph.bank_of[kind]][:].rearrange("p (c o) -> p c o", c=KC),
                                                main[a][:], ALU.add).then_inc(free[ph.bank_of[kind]], 1)
                    return f

                def statistics(kind, src, at):
                    def f(m, value, _):
                        link, done = linker(value, (kind + "s", 0))
                        if kind == "pn":
                            dve.wait_ge(s["pe_added"], value(lambda m: m + 1))
                        else:
                            dve.wait_ge(free[ph.bank_of["o1"]], value(use("o1")))
                            dve.wait_ge(free[ph.bank_of["o0"]], value(use("o0")))
                        for i in range(NT):
                            ins = nc.vector.bn_stats(stats[kind][:, i, :], src[:, i, :])
                        link(ins)
                        for i in range(NT):
                            ins = nc.vector.bn_aggr(aggr[:, at + i, :], stats[kind][:, i, :])
                        ins.then_inc(s["chain"], 1)
                    return f

                def inverse_root(n, value, i):
                    dve.wait_ge(s["chain"], value(lambda n: ph.chained["nm", n, i - 1] + 1 if i else ph.chained["nm", n, 0]))
                    var = root[:, 3, :]
                    steps = [lambda: nc.vector.tensor_scalar(var, aggr[:, :, 1], EPS, None, ALU.add)]
                    steps += rsqrt_steps(nc.vector, root[:, 0, :], var, root[:, 1, :], root[:, 2, :])
                    assert len(steps) == ROOT_STEPS
                    steps[i]().then_inc(s["chain"], 1)

                def normalise_rows(kind, src, dst, at, done_sem):
                    def f(m, value, _):
                        back = 2 if kind == "pn" else -1
                        dve.wait_ge(s["chain"], value(lambda m: ph.chained["nm", m - back, ROOT_STEPS - 1] + 1))
                        if kind == "pn":
                            if not isinstance(m, int) or m > 0:
                                dve.wait_ge(ready[ph.bank_of["t1"]], value(lambda m: ph.use["t1", m - 1, 0]))
                        elif not isinstance(m, int) or m > 0:
                            dve.wait_ge(d_out2, value(lambda m: 16 * m))
                            dve.wait_ge(ready[ph.bank_of["pl"]], value(lambda m: ph.use["pl", m - 1, 0]))
                        for i in range(NT):
                            ins = nc.vector.tensor_scalar(dst[:, i, :], src[:, i, :], aggr[:, at + i, 0:1], root[:, 0, at + i:at + i + 1],
                                                          ALU.subtract, ALU.mult)
                        ins.then_inc(done_sem, 1)
                    return f

                def pool_tokens(m, value, _):
                    wait_bank(dve, value, "pl")
                    nc.vector.tensor_tensor(pooled[:].rearrange("p c b -> p (c b)"), bank[ph.bank_of["pl"]][:, 0:KC * BATCH],
                                            pooled[:].rearrange("p c b -> p (c b)"), ALU.add).then_inc(free[ph.bank_of["pl"]], 1)

                h = dict(M=maximum, m=max_rows, x=normalise, q0=rest_part("q", 0), k0=rest_part("k", 0), q1=rest_part("q", 1),
                         k1=rest_part("k", 1), v0=take_values("v0", 0), v1=take_values("v1", 1), o0=add_residual("o0", 0),
                         o1=add_residual("o1", 1), wq=experts("q"), wk=experts("k"), wv=experts("v"), wo=experts("o"), pl=pool_tokens)
                if not second:
                    h |= dict(pns=statistics("pn", emb_t, 0), pna=normalise_rows("pn", emb_t, xn, 0, s["xn_ready"]),
                              lns=statistics("ln", hout, NT), lna=normalise_rows("ln", hout, hnew, NT, s["hnew_ready"]),
                              nm=inverse_root)
                ph.run(dve, h)

            @block.gpsimd
            def _(pool):
                def low_part(a):
                    def f(m, value, c):
                        hold(pool, s["qk_rest"], value(lambda m: 4 * m + piece[f"{a}{c}"]))
                        nc.gpsimd.tensor_tensor(part[a, c, 2][:], rest[a][:], part[a, c, 1][:], ALU.subtract).then_inc(s["qk_parts"], 1)
                    return f

                def copy_values(m, value, g):
                    hold(pool, free[ph.bank_of["v1"]], value(use("v1")))
                    if not isinstance(m, int) or m > 0:
                        hold(pool, s["pv_done"], value(lambda m: (slot(m - 1, g) + 1) * ph.steps))
                    for i in range(NT):
                        ins = nc.gpsimd.tensor_copy(vp[:, i, g * GH:(g + 1) * GH, 0:HD],
                                                    vs[:, i, g * 64:(g + 1) * 64].rearrange("p (j e) -> p j e", j=GH))
                    ins.then_inc(s["v_copied"], 1)

                def residual_bias(m, value, _):
                    hold(pool, d_res, value(lambda m: 16 * (m + 1)))
                    nc.gpsimd.tensor_tensor(res[:], res[:], bias_row[fam, "o"][:].unsqueeze(1).to_broadcast([P, NT, D]), ALU.add).then_inc(s["res_ready"], 1)

                def scale_factor(a):
                    def f(m, value, _):
                        if value(lambda m: uc_count(m, a)) != 1 if isinstance(m, int) else True:
                            if not isinstance(m, int) or m > 0:
                                hold(pool, ready[ph.bank_of["w" + a]], value(lambda m: ph.use["w" + a, m - 1, 0]))
                        i = "qkvo".index(a)
                        nc.gpsimd.tensor_copy(coef_b[a][:], coef[:, bass.ds(m, 1), i:i + 1].rearrange("p b x -> p (b x)")).then_inc(s["coef_ready"], 1)
                        hold(pool, s["coef_ready"], value(lambda m: uc_count(m, a)))
                        nc.gpsimd.tensor_scalar(uc[a][:], uall[a][:], coef_b[a][:, 0:1], None, ALU.mult).then_inc(s["uc_ready"], 1)
                    return f

                def embed(m, value, _):
                    hold(pool, d_idx, value(lambda m: 16 * (m + 1)))
                    if not isinstance(m, int) or m > 0:
                        hold(pool, s["xn_ready"], value(lambda m: m))
                        hold(pool, d_h0, value(lambda m: 16 * m))
                    for i in range(NT):
                        pool.indirect_dma_start(out=emb_t[:, i, :], out_offset=None, in_=io["emb"],
                                                in_offset=bass.IndirectOffsetOnAxis(ap=idx_t[:, i:i + 1], axis=0)).then_inc(d_x, 16)

                def add_positions(m, value, _):
                    hold(pool, d_x, value(lambda m: 64 * (m + 1)))
                    hold(pool, d_pe, value(lambda m: 16 * (m + 1)))
                    nc.gpsimd.tensor_tensor(emb_t[:], emb_t[:], pe_t[:], ALU.add).then_inc(s["pe_added"], 1)

                h = dict(qm=low_part("q"), km=low_part("k"), vc=copy_values,
                         rb=residual_bias)
                if second:
                    h |= {"w" + a: scale_factor(a) for a in "qkvo"}
                else:
                    h |= dict(pg=embed, pa=add_positions)
                ph.run(pool, h)

            @block.sync
            def _(sp):
                def write_stack(m, value, c):
                    hold(sp, s["qk_parts"], value(lambda m: 4 * m + 2 * c + 2))
                    if not isinstance(m, int) or m > 0:
                        for g in (2 * c, 2 * c + 1):
                            hold(sp, d_read[g], value(lambda m: 32 * m))
                    for a in "qk":
                        for i in range(3):
                            first, times = PARTS[a].index(i), PARTS[a].count(i)
                            step = PARTS[a].index(i, first + 1) - first if times > 1 else 1
                            rows = stack_dram[a][c, :, first:first + (times - 1) * step + 1:step, :]
                            sp.dma_start(rows, part[a, c, i][:].unsqueeze(1).to_broadcast([P, times, TOK])).then_inc(d_write[c], 16)

                def read_stack(m, value, g):
                    c, heads = g // 2, slice(4 * (g % 2), 4 * (g % 2) + 4)
                    hold(sp, d_write[c], value(lambda m: 96 * (m + 1)))
                    if not isinstance(m, int) or m > 0:
                        hold(sp, s["score_ready"], value(lambda m: (slot(m - 1, g) + 1) * NB))
                    for a, stack in (("k", kstack), ("q", qstack)):
                        rows = stack_dram[a][c].rearrange("(h e) r t -> (e r) h t", h=8)
                        sp.dma_start(stack[0:SPLIT, g], rows[:, heads, :]).then_inc(d_read[g], 16)

                def load_residual(m, value, _):
                    if not isinstance(m, int) or m > 0:
                        hold(sp, free[ph.bank_of["o1"]], value(lambda m: ph.use["o1", m - 1, 0]))
                    if second:
                        src = by_batch(h1_dram)
                    else:
                        src = h0_dram
                        hold(sp, d_h0, value(lambda m: 16 * (m + 1)))
                    sp.dma_start(res[:], src[m]).then_inc(d_res, 16)

                def prepare(m, value, _):
                    if second:
                        if not isinstance(m, int) or m > 0:
                            hold(sp, ready[ph.bank_of["t1"]], value(lambda m: ph.use["t1", m - 1, 0]))
                        sp.dma_start(xn[:], by_batch(xn_dram)[m]).then_inc(d_x, 16)
                        return
                    if not isinstance(m, int) or m > 0:
                        hold(sp, d_x, value(lambda m: 64 * m))
                        hold(sp, s["pe_added"], value(lambda m: m))
                    sp.dma_start(idx_t[:], io["tokens"][m]).then_inc(d_idx, 16)
                    sp.dma_start(pe_t[:], io["c_pe"][m]).then_inc(d_pe, 16)

                def store_embedded(m, value, _):
                    hold(sp, s["pe_added"], value(lambda m: m + 1))
                    sp.dma_start(h0_dram[m], emb_t[:]).then_inc(d_h0, 16)

                def store(m, value, _):
                    hold(sp, free[ph.bank_of["o1"]], value(use("o1")))
                    hold(sp, free[ph.bank_of["o0"]], value(use("o0")))
                    if second:
                        sp.dma_start(out[m].rearrange("(i p) c -> p i c", p=P), hout[:]).then_inc(d_out, 16)
                    else:
                        sp.dma_start(by_item(h1_dram)[m], hout[:]).then_inc(d_out, 16)

                def store_normalised(m, value, _):
                    hold(sp, s["hnew_ready"], value(lambda m: m + 1))
                    sp.dma_start(by_item(xn_dram)[m], hnew[:]).then_inc(d_out2, 16)

                h = dict(sw=write_stack, sr=read_stack, rs=load_residual, prep=prepare, st=store)
                if not second:
                    h |= dict(ps=store_embedded, s2=store_normalised)
                ph.run(sp, h)
                hold(sp, d_out, 16 * ITEMS)
                if not second:
                    hold(sp, d_out2, 16 * ITEMS)

    def gating():
        gw1 = sb("gw1", [P, KC, GATE_H], F32)
        gb1 = sb("gb1", [GATE_H, 1], F32)
        gw2 = sb("gw2", [GATE_H, EXPERTS], F32)
        gb2 = sb("gb2", [BATCH, EXPERTS], F32)
        number = sb("number", [BATCH, EXPERTS], F32)
        spread = sb("spread", [EXPERTS, P], F32)
        hid = sb("hid", [GATE_H, BATCH], F32)
        logit = sb("logit", [BATCH, EXPERTS], F32)
        top = sb("top", [BATCH, 8], F32)
        topi = sb("topi", [BATCH, 8], U32)
        topf = sb("topf", [BATCH, 8], F32)
        e2 = sb("e2", [BATCH, 4], F32)
        gate = sb("gate", [BATCH, 2, EXPERTS], F32)
        gateT = sb("gateT", [EXPERTS, BATCH], F32)
        s_l, s_p, s_v, s_a = sem("g_loads"), sem("g_products"), sem("g_vector"), sem("g_exp")
        with nc.Block() as block:
            @block.sync
            def _(sp):
                loads = [(gw1[:], io["g_w1T"].rearrange("(c p) g -> p c g", p=P)), (gb1[:], io["g_b1"]), (gw2[:], io["g_w2T"]),
                         (gb2[:], io["g_b2"].to_broadcast([BATCH, EXPERTS])), (number[:], io["c_number"]), (spread[:], io["c_spread"])]
                for to, of in loads:
                    sp.dma_start(to, of).then_inc(s_l, 16)
                sp.wait_ge(s_late, setup.later)
                gating.loads = 16 * len(loads)

            @block.tensor
            def _(pe):
                pe.wait_ge(s_l, gating.loads)
                for c in range(KC):
                    last = nc.tensor.matmul(sc[0][0:GATE_H, 0:BATCH], gw1[:, c, :], pooled[:, c, :], start=(c == 0), stop=(c == KC - 1))
                last.then_inc(s_p, 1)
                pe.wait_ge(s_v, 1)
                nc.tensor.matmul(sc[1][0:BATCH, 0:EXPERTS], hid[:], gw2[:], start=True, stop=True).then_inc(s_p, 1)
                pe.wait_ge(s_v, 12)
                nc.tensor.transpose(mx[0][0:EXPERTS, 0:BATCH], gate[:, 0, :], ident[0:BATCH, 0:BATCH]).then_inc(s_p, 1)
                pe.wait_ge(s_v, 13)
                nc.tensor.matmul(mx[1][:, 0:BATCH], spread[:], gateT[:], start=True, stop=True).then_inc(s_p, 1)

            @block.scalar
            def _(act):
                act.wait_ge(s_v, 4)
                nc.scalar.activation(e2[:, 1:2], e2[:, 0:1], ACT.Exp).then_inc(s_a, 1)

            @block.vector
            def _(dve):
                v = nc.vector
                links = [0]

                def link(ins):
                    links[0] += 1
                    ins.then_inc(s_v, 1)
                    dve.wait_ge(s_v, links[0])

                dve.wait_ge(s_late, setup.later)
                v.memset(qstack[MASK0:MAX0], 0.0)
                dve.wait_ge(s_l, gating.loads)
                dve.wait_ge(s_p, 1)
                link(v.tensor_scalar(hid[:], sc[0][0:GATE_H, 0:BATCH], gb1[:, 0:1], 0.0, ALU.add, ALU.max))
                dve.wait_ge(s_p, 2)
                link(v.tensor_tensor(logit[:], sc[1][0:BATCH, 0:EXPERTS], gb2[:], ALU.add))
                link(v.max(top[:], logit[:]))
                link(v.tensor_tensor(e2[:, 0:1], top[:, 1:2], top[:, 0:1], ALU.subtract))
                link(v.max_index(topi[:], top[:], logit[:]))
                link(v.tensor_copy(topf[:], topi[:]))
                dve.wait_ge(s_a, 1)
                link(v.tensor_scalar(e2[:, 2:3], e2[:, 1:2], 1.0, None, ALU.add))
                link(v.reciprocal(e2[:, 0:1], e2[:, 2:3]))
                link(v.tensor_tensor(e2[:, 1:2], e2[:, 1:2], e2[:, 0:1], ALU.mult))
                for i in range(2):
                    link(v.tensor_scalar(gate[:, i, :], number[:], topf[:, i:i + 1], e2[:, i:i + 1], ALU.is_equal, ALU.mult))
                link(v.tensor_tensor(gate[:, 0, :], gate[:, 0, :], gate[:, 1, :], ALU.add))
                dve.wait_ge(s_p, 3)
                link(v.tensor_copy(gateT[:], mx[0][0:EXPERTS, 0:BATCH]))
                dve.wait_ge(s_p, 4)
                for i in range(4):
                    link(v.tensor_scalar(coef[:, :, i], mx[1][:, 0:BATCH], sall[:, i:i + 1], None, ALU.mult))

    setup()
    attention(False)
    gating()
    attention(True)


def positions():
    pos = np.arange(SEQ, dtype=np.float32)[:, None]
    i = np.arange(D)
    denom = np.power(np.float32(10000.0), (2 * (i // 2)).astype(np.float32) / np.float32(D), dtype=np.float32)
    angle = (pos / denom).astype(np.float32)
    return np.where(i % 2 == 0, np.sin(angle), np.cos(angle)).astype(np.float32)


def kernel(**inputs):
    import concourse.bacc as _bacc
    from concourse.bass_utils import run_bass_kernel_spmd as _run

    a = {k: np.asarray(v) for k, v in inputs.items()}
    lay = {}
    lay["tokens"] = a["x"].T.reshape(ITEMS, NT, P).transpose(0, 2, 1)
    lay["emb"] = a["L0_tok_emb"]
    for p in "qv":
        lay[f"a_dir_{p}T"] = a[f"L0_attn_dir_{p}"].T
        lay[f"a_A_{p}"] = a[f"L0_attn_A_{p}"]
        lay[f"a_B_{p}T"] = a[f"L0_attn_B_{p}"].T
        lay[f"a_mag_{p}"] = a[f"L0_attn_mag_{p}"].reshape(1, 1)
        lay[f"a_b{p}"] = a[f"L0_attn_bias_{p}"]
    lay["a_k_wT"], lay["a_bk"] = a["L0_attn_k_w"].T, a["L0_attn_k_b"]
    lay["a_out_wT"], lay["a_bo"] = a["L0_attn_out_w"].T, a["L0_attn_out_b"]
    for p in "qkvo":
        lay[f"f_{p}WmT"] = a[f"L0_ffn_{p}Wm"].T
        lay[f"f_{p}V"] = a[f"L0_ffn_{p}V"].reshape(P, D)
        lay[f"f_{p}UT"] = a[f"L0_ffn_{p}U"].transpose(0, 2, 1).reshape(P, D)
        lay[f"f_{p}S"] = a[f"L0_ffn_{p}S"].reshape(P, 1)
        lay[f"f_b{p}"] = a[f"L0_ffn_{p}b"]
    lay["g_w1T"], lay["g_b1"] = a["L0_ffn_gw1"].T, a["L0_ffn_gb1"].reshape(GATE_H, 1)
    lay["g_w2T"], lay["g_b2"] = a["L0_ffn_gw2"].T, a["L0_ffn_gb2"].reshape(1, EXPERTS)
    own = np.arange(TOK)[None, :] % P // BATCH == np.arange(P // BATCH)[:, None]
    lay["c_mask"] = np.stack([own, np.where(own, 0.0, -FAR)], axis=1).astype(np.float32)
    lay["c_ident"] = np.eye(P, dtype=np.float32)
    lay["c_mean"] = np.tile(np.eye(BATCH, dtype=np.float32) / SEQ, (P // BATCH, 1))
    lay["c_pe"] = np.repeat(positions(), BATCH, axis=0).reshape(ITEMS, NT, P, D).transpose(0, 2, 1, 3)
    lay["c_number"] = np.tile(np.arange(EXPERTS, dtype=np.float32), (BATCH, 1))
    lay["c_spread"] = np.repeat(np.eye(EXPERTS, dtype=np.float32), RANK, axis=1)

    nc = _bacc.Bacc("TRN2", target_bir_lowering=False, num_devices=1)
    arrays, io = {}, {}
    for name, v in lay.items():
        v = np.ascontiguousarray(v)
        arrays[f"in_{name}"] = v
        io[name] = nc.dram_tensor(f"in_{name}", v.shape, mybir.dt.from_np(v.dtype), kind="ExternalInput").ap()
    out = nc.dram_tensor("out_0", (BATCH, SEQ, D), F32, kind="ExternalOutput").ap()
    with ExitStack() as ctx:
        tower(nc, ctx, io, out)
    r = _run(nc, [arrays], core_ids=[0])
    return r.results[0]["out_0"]
```
